# Optimizing a Trainium2 kernel written in Bass

```python
import numpy as np
import jax
import jax.numpy as jnp

def _softmax(x, axis=-1):
    return jax.nn.softmax(x, axis=axis)

def _gelu(x):
    return jax.nn.gelu(x, approximate=True)

def _silu(x):
    return jax.nn.silu(x)

def _sigmoid(x):
    return jax.nn.sigmoid(x)

def _layernorm(x, axis=-1, eps=1e-05):
    m = jnp.mean(x, axis=axis, keepdims=True)
    v = jnp.var(x, axis=axis, keepdims=True)
    return (x - m) / jnp.sqrt(v + eps)

def _scatter_add(tgt, idx, src, axis=0):
    return tgt.at[idx].add(src)

def _segment_sum(src, seg, n):
    return jax.ops.segment_sum(src, seg, n)
kernel_name = 'mk_dlrm_tower_d1_rec_r8_92a173'

def setup_inputs(seed: int=0):
    np.random.seed(seed)
    _w = jnp.asarray

    def _rec_inputs():
        import jax
        import jax.numpy as jnp
        _tk = jax.random.key(seed)
        dense_ctx = jax.random.normal(jax.random.fold_in(_tk, 190), (1024, 16), jnp.float32)
        ids = jnp.stack([jax.random.randint(jax.random.fold_in(_tk, 200 + f), (1024,), 0, v, jnp.int32) for f, v in enumerate([125000, 125000, 125000, 1000, 125000, 1250, 12500, 12500, 1000, 125000, 1250, 1000, 1000, 1250, 1250, 1250, 125000, 12500, 12500, 125000, 1250, 12500, 1250, 1250, 1250, 1250, 125000, 12500, 125000, 1250, 12500, 125000, 1250, 1000, 125000, 125000, 1250, 1000, 125000])], axis=1)
        tbl_0 = 0.05 * jax.random.normal(jax.random.fold_in(_tk, 500 + 0), (125000, 16), jnp.float32)
        tbl_1 = 0.05 * jax.random.normal(jax.random.fold_in(_tk, 500 + 1), (125000, 16), jnp.float32)
        tbl_2 = 0.05 * jax.random.normal(jax.random.fold_in(_tk, 500 + 2), (125000, 16), jnp.float32)
        tbl_3 = 0.05 * jax.random.normal(jax.random.fold_in(_tk, 500 + 3), (1000, 16), jnp.float32)
        tbl_4 = 0.05 * jax.random.normal(jax.random.fold_in(_tk, 500 + 4), (125000, 16), jnp.float32)
        tbl_5 = 0.05 * jax.random.normal(jax.random.fold_in(_tk, 500 + 5), (1250, 16), jnp.float32)
        tbl_6 = 0.05 * jax.random.normal(jax.random.fold_in(_tk, 500 + 6), (12500, 16), jnp.float32)
        tbl_7 = 0.05 * jax.random.normal(jax.random.fold_in(_tk, 500 + 7), (12500, 16), jnp.float32)
        tbl_8 = 0.05 * jax.random.normal(jax.random.fold_in(_tk, 500 + 8), (1000, 16), jnp.float32)
        tbl_9 = 0.05 * jax.random.normal(jax.random.fold_in(_tk, 500 + 9), (125000, 16), jnp.float32)
        tbl_10 = 0.05 * jax.random.normal(jax.random.fold_in(_tk, 500 + 10), (1250, 16), jnp.float32)
        tbl_11 = 0.05 * jax.random.normal(jax.random.fold_in(_tk, 500 + 11), (1000, 16), jnp.float32)
        tbl_12 = 0.05 * jax.random.normal(jax.random.fold_in(_tk, 500 + 12), (1000, 16), jnp.float32)
        tbl_13 = 0.05 * jax.random.normal(jax.random.fold_in(_tk, 500 + 13), (1250, 16), jnp.float32)
        tbl_14 = 0.05 * jax.random.normal(jax.random.fold_in(_tk, 500 + 14), (1250, 16), jnp.float32)
        tbl_15 = 0.05 * jax.random.normal(jax.random.fold_in(_tk, 500 + 15), (1250, 16), jnp.float32)
        tbl_16 = 0.05 * jax.random.normal(jax.random.fold_in(_tk, 500 + 16), (125000, 16), jnp.float32)
        tbl_17 = 0.05 * jax.random.normal(jax.random.fold_in(_tk, 500 + 17), (12500, 16), jnp.float32)
        tbl_18 = 0.05 * jax.random.normal(jax.random.fold_in(_tk, 500 + 18), (12500, 16), jnp.float32)
        tbl_19 = 0.05 * jax.random.normal(jax.random.fold_in(_tk, 500 + 19), (125000, 16), jnp.float32)
        tbl_20 = 0.05 * jax.random.normal(jax.random.fold_in(_tk, 500 + 20), (1250, 16), jnp.float32)
        tbl_21 = 0.05 * jax.random.normal(jax.random.fold_in(_tk, 500 + 21), (12500, 16), jnp.float32)
        tbl_22 = 0.05 * jax.random.normal(jax.random.fold_in(_tk, 500 + 22), (1250, 16), jnp.float32)
        tbl_23 = 0.05 * jax.random.normal(jax.random.fold_in(_tk, 500 + 23), (1250, 16), jnp.float32)
        tbl_24 = 0.05 * jax.random.normal(jax.random.fold_in(_tk, 500 + 24), (1250, 16), jnp.float32)
        tbl_25 = 0.05 * jax.random.normal(jax.random.fold_in(_tk, 500 + 25), (1250, 16), jnp.float32)
        tbl_26 = 0.05 * jax.random.normal(jax.random.fold_in(_tk, 500 + 26), (125000, 16), jnp.float32)
        tbl_27 = 0.05 * jax.random.normal(jax.random.fold_in(_tk, 500 + 27), (12500, 16), jnp.float32)
        tbl_28 = 0.05 * jax.random.normal(jax.random.fold_in(_tk, 500 + 28), (125000, 16), jnp.float32)
        tbl_29 = 0.05 * jax.random.normal(jax.random.fold_in(_tk, 500 + 29), (1250, 16), jnp.float32)
        tbl_30 = 0.05 * jax.random.normal(jax.random.fold_in(_tk, 500 + 30), (12500, 16), jnp.float32)
        tbl_31 = 0.05 * jax.random.normal(jax.random.fold_in(_tk, 500 + 31), (125000, 16), jnp.float32)
        tbl_32 = 0.05 * jax.random.normal(jax.random.fold_in(_tk, 500 + 32), (1250, 16), jnp.float32)
        tbl_33 = 0.05 * jax.random.normal(jax.random.fold_in(_tk, 500 + 33), (1000, 16), jnp.float32)
        tbl_34 = 0.05 * jax.random.normal(jax.random.fold_in(_tk, 500 + 34), (125000, 16), jnp.float32)
        tbl_35 = 0.05 * jax.random.normal(jax.random.fold_in(_tk, 500 + 35), (125000, 16), jnp.float32)
        tbl_36 = 0.05 * jax.random.normal(jax.random.fold_in(_tk, 500 + 36), (1250, 16), jnp.float32)
        tbl_37 = 0.05 * jax.random.normal(jax.random.fold_in(_tk, 500 + 37), (1000, 16), jnp.float32)
        tbl_38 = 0.05 * jax.random.normal(jax.random.fold_in(_tk, 500 + 38), (125000, 16), jnp.float32)
        _rk = jax.random.fold_in(_tk, 7)
        W_top1 = 0.05 * jax.random.normal(jax.random.fold_in(_tk, 801), (400, 512), jnp.float32)
        W_top2 = 0.0441942 * jax.random.normal(jax.random.fold_in(_tk, 802), (512, 256), jnp.float32)
        W_top3 = 0.0625 * jax.random.normal(jax.random.fold_in(_tk, 803), (256, 1), jnp.float32)
        b_top1 = jnp.zeros((512,), jnp.float32)
        b_top2 = jnp.zeros((256,), jnp.float32)
        return (dense_ctx, ids, tbl_0, tbl_1, tbl_2, tbl_3, tbl_4, tbl_5, tbl_6, tbl_7, tbl_8, tbl_9, tbl_10, tbl_11, tbl_12, tbl_13, tbl_14, tbl_15, tbl_16, tbl_17, tbl_18, tbl_19, tbl_20, tbl_21, tbl_22, tbl_23, tbl_24, tbl_25, tbl_26, tbl_27, tbl_28, tbl_29, tbl_30, tbl_31, tbl_32, tbl_33, tbl_34, tbl_35, tbl_36, tbl_37, tbl_38, W_top1, b_top1, W_top2, b_top2, W_top3)
    dense_ctx, ids, tbl_0, tbl_1, tbl_2, tbl_3, tbl_4, tbl_5, tbl_6, tbl_7, tbl_8, tbl_9, tbl_10, tbl_11, tbl_12, tbl_13, tbl_14, tbl_15, tbl_16, tbl_17, tbl_18, tbl_19, tbl_20, tbl_21, tbl_22, tbl_23, tbl_24, tbl_25, tbl_26, tbl_27, tbl_28, tbl_29, tbl_30, tbl_31, tbl_32, tbl_33, tbl_34, tbl_35, tbl_36, tbl_37, tbl_38, W_top1, b_top1, W_top2, b_top2, W_top3 = _rec_inputs()

    def _L0_rec_setup():
        import jax, jax.numpy as jnp
        import numpy as np
        B, F0, D = (512, 39, 16)
        CIN = [128, 128, 128]

        def _cin_layer(X0, Xi, W, b):
            H = W.shape[0]
            F0_, Fi = (X0.shape[1], Xi.shape[1])
            Wr = W.reshape(H, F0_, Fi)
            return jnp.einsum('hjk,bjd,bkd->bhd', Wr, X0, Xi) + b[None, :, None]
        key = jax.random.key(seed)
        ks = jax.random.split(key, 4)
        x = jax.random.normal(ks[0], (B, F0, D), dtype=jnp.float32)
        fields = [F0] + CIN
        inp = {'embedded_features': x}
        for i in range(len(CIN)):
            cin = F0 * fields[i]
            cout = fields[i + 1]
            kw = jax.random.fold_in(ks[1], i)
            inp[f'W{i}'] = jax.random.normal(kw, (cout, cin), dtype=jnp.float32) / np.sqrt(cin)
            inp[f'b{i}'] = jnp.zeros((cout,), dtype=jnp.float32)
        return inp
    _L0_rec_all = _L0_rec_setup()
    _L0_rec_in = {k: v for k, v in _L0_rec_all.items() if k in ('W0', 'b0', 'W1', 'b1', 'W2', 'b2')}
    del _L0_rec_all
    return {'dense_ctx': dense_ctx, 'ids': ids, 'tbl_0': tbl_0, 'tbl_1': tbl_1, 'tbl_2': tbl_2, 'tbl_3': tbl_3, 'tbl_4': tbl_4, 'tbl_5': tbl_5, 'tbl_6': tbl_6, 'tbl_7': tbl_7, 'tbl_8': tbl_8, 'tbl_9': tbl_9, 'tbl_10': tbl_10, 'tbl_11': tbl_11, 'tbl_12': tbl_12, 'tbl_13': tbl_13, 'tbl_14': tbl_14, 'tbl_15': tbl_15, 'tbl_16': tbl_16, 'tbl_17': tbl_17, 'tbl_18': tbl_18, 'tbl_19': tbl_19, 'tbl_20': tbl_20, 'tbl_21': tbl_21, 'tbl_22': tbl_22, 'tbl_23': tbl_23, 'tbl_24': tbl_24, 'tbl_25': tbl_25, 'tbl_26': tbl_26, 'tbl_27': tbl_27, 'tbl_28': tbl_28, 'tbl_29': tbl_29, 'tbl_30': tbl_30, 'tbl_31': tbl_31, 'tbl_32': tbl_32, 'tbl_33': tbl_33, 'tbl_34': tbl_34, 'tbl_35': tbl_35, 'tbl_36': tbl_36, 'tbl_37': tbl_37, 'tbl_38': tbl_38, 'W_top1': W_top1, 'b_top1': b_top1, 'W_top2': W_top2, 'b_top2': b_top2, 'W_top3': W_top3, 'L0_rec_W0': _L0_rec_in['W0'], 'L0_rec_b0': _L0_rec_in['b0'], 'L0_rec_W1': _L0_rec_in['W1'], 'L0_rec_b1': _L0_rec_in['b1'], 'L0_rec_W2': _L0_rec_in['W2'], 'L0_rec_b2': _L0_rec_in['b2']}

def reference(dense_ctx, ids, tbl_0, tbl_1, tbl_2, tbl_3, tbl_4, tbl_5, tbl_6, tbl_7, tbl_8, tbl_9, tbl_10, tbl_11, tbl_12, tbl_13, tbl_14, tbl_15, tbl_16, tbl_17, tbl_18, tbl_19, tbl_20, tbl_21, tbl_22, tbl_23, tbl_24, tbl_25, tbl_26, tbl_27, tbl_28, tbl_29, tbl_30, tbl_31, tbl_32, tbl_33, tbl_34, tbl_35, tbl_36, tbl_37, tbl_38, W_top1, b_top1, W_top2, b_top2, W_top3, L0_rec_W0, L0_rec_b0, L0_rec_W1, L0_rec_b1, L0_rec_W2, L0_rec_b2):
    import jax
    import jax.numpy as jnp

    def _L0_rec_ref(embedded_features, W0, b0, W1, b1, W2, b2):
        import jax, jax.numpy as jnp
        import numpy as np
        B, F0, D = (512, 39, 16)
        CIN = [128, 128, 128]

        def _cin_layer(X0, Xi, W, b):
            H = W.shape[0]
            F0_, Fi = (X0.shape[1], Xi.shape[1])
            Wr = W.reshape(H, F0_, Fi)
            return jnp.einsum('hjk,bjd,bkd->bhd', Wr, X0, Xi) + b[None, :, None]
        X0 = embedded_features
        Ws = [(W0, b0), (W1, b1), (W2, b2)]
        Xi = X0
        res = []
        for W, b in Ws:
            Xi = _cin_layer(X0, Xi, W, b)
            res.append(Xi.sum(axis=2))
        return jnp.concatenate(res, axis=1)
    e = jnp.stack([tbl_0[ids[:, 0]], tbl_1[ids[:, 1]], tbl_2[ids[:, 2]], tbl_3[ids[:, 3]], tbl_4[ids[:, 4]], tbl_5[ids[:, 5]], tbl_6[ids[:, 6]], tbl_7[ids[:, 7]], tbl_8[ids[:, 8]], tbl_9[ids[:, 9]], tbl_10[ids[:, 10]], tbl_11[ids[:, 11]], tbl_12[ids[:, 12]], tbl_13[ids[:, 13]], tbl_14[ids[:, 14]], tbl_15[ids[:, 15]], tbl_16[ids[:, 16]], tbl_17[ids[:, 17]], tbl_18[ids[:, 18]], tbl_19[ids[:, 19]], tbl_20[ids[:, 20]], tbl_21[ids[:, 21]], tbl_22[ids[:, 22]], tbl_23[ids[:, 23]], tbl_24[ids[:, 24]], tbl_25[ids[:, 25]], tbl_26[ids[:, 26]], tbl_27[ids[:, 27]], tbl_28[ids[:, 28]], tbl_29[ids[:, 29]], tbl_30[ids[:, 30]], tbl_31[ids[:, 31]], tbl_32[ids[:, 32]], tbl_33[ids[:, 33]], tbl_34[ids[:, 34]], tbl_35[ids[:, 35]], tbl_36[ids[:, 36]], tbl_37[ids[:, 37]], tbl_38[ids[:, 38]]], axis=1)
    z = _L0_rec_ref(e, L0_rec_W0, L0_rec_b0, L0_rec_W1, L0_rec_b1, L0_rec_W2, L0_rec_b2)
    z = z.reshape(z.shape[0], -1)
    h = jnp.concatenate([z, dense_ctx], axis=1)
    h = jnp.maximum(h @ W_top1 + b_top1, 0.0)
    h = jnp.maximum(h @ W_top2 + b_top2, 0.0)
    y = h @ W_top3
    return y

_drawn_inputs = setup_inputs


def setup_inputs(seed=0):
    import zlib

    import numpy as np

    out = dict(_drawn_inputs(seed))
    spreads = {'b_top1': (0.0, 0.1),
     'b_top2': (0.0, 0.1),
     'L0_rec_b0': (0.0, 0.1),
     'L0_rec_b1': (0.0, 0.1),
     'L0_rec_b2': (0.0, 0.1)}
    factors = {'tbl_0': 8.0,
     'tbl_1': 5.721,
     'tbl_2': 5.342,
     'tbl_3': 6.964,
     'tbl_4': 8.0,
     'tbl_5': 8.0,
     'tbl_6': 8.0,
     'tbl_7': 6.749,
     'tbl_8': 8.0,
     'tbl_9': 8.0,
     'tbl_10': 8.0,
     'tbl_11': 6.948,
     'tbl_12': 8.0,
     'tbl_13': 8.0,
     'tbl_14': 4.183,
     'tbl_15': 5.748,
     'tbl_16': 8.0,
     'tbl_17': 8.0,
     'tbl_18': 8.0,
     'tbl_19': 5.824,
     'tbl_20': 6.889,
     'tbl_21': 8.0,
     'tbl_22': 8.0,
     'tbl_23': 8.0,
     'tbl_24': 8.0,
     'tbl_25': 7.068,
     'tbl_26': 6.196,
     'tbl_27': 8.0,
     'tbl_28': 8.0,
     'tbl_29': 8.0,
     'tbl_30': 6.558,
     'tbl_31': 6.503,
     'tbl_32': 8.0,
     'tbl_33': 6.402,
     'tbl_34': 8.0,
     'tbl_35': 7.539,
     'tbl_36': 8.0,
     'tbl_37': 6.585,
     'tbl_38': 8.0,
     'L0_rec_W0': 3.026}
    for name, (base, spread) in spreads.items():
        noise = np.random.default_rng([zlib.crc32(name.encode()), seed]).standard_normal(out[name].shape)
        drawn = base * np.exp(spread * noise) if base else spread * noise
        out[name] = jnp.asarray(drawn.astype(out[name].dtype))
    for name, factor in factors.items():
        out[name] = (out[name] * factor).astype(out[name].dtype)
    return out
```

```python
from contextlib import ExitStack

import numpy as np
import concourse.bass as bass
from concourse import mybir

F32 = mybir.dt.float32
F32R = mybir.dt.float32r
I32 = mybir.dt.int32
U32 = mybir.dt.uint32
ALU = mybir.AluOpType
ACT = mybir.ActivationFunctionType
AX = mybir.AxisListType

P = 128
NF = 39
D = 16
H = 128
B = 1024
GROUP = 128
GROUPS = B // GROUP
BLOCK = 32
BLOCKS = GROUP // BLOCK
COLS = BLOCK * D
TILE = P // D
TILES = BLOCK // TILE
PAIRS = TILES // 2
CHUNKS = 10
STEPS = PAIRS * CHUNKS
SHIFTS = NF // 2 + 1
ROWS0 = 3 * NF
CHUNKS0 = -(-SHIFTS // 3)
LO = 64
SELK = LO + NF
NP2 = NF + 1

FIELDS = [range(4 * c, min(4 * c + 4, NF)) for c in range(CHUNKS)]
ACT_CHUNKS = (3, 7)
TERMS = sum(len(FIELDS[c]) for c in ACT_CHUNKS)
DVE_UPTO, ACT_UPTO = [0], [0]
for c, f in enumerate(FIELDS):
    DVE_UPTO.append(DVE_UPTO[-1] + 2 * len(f) * (c not in ACT_CHUNKS))
    ACT_UPTO.append(ACT_UPTO[-1] + 2 * len(f) * (c in ACT_CHUNKS))
PER_PAIR = DVE_UPTO[-1]
GATHERS = 8


def rows0(c):
    return NF * min(3, SHIFTS - 3 * c)


def build(nc, t):
    ctx = ExitStack()
    with ctx:
        def sb(name, shape, dt=F32):
            return ctx.enter_context(nc.sbuf_tensor(name, shape, dt))

        def ps(name, shape):
            return ctx.enter_context(nc.psum_tensor(name, shape, F32))

        def sem(name):
            return ctx.enter_context(nc.semaphore(name))

        w1_hi = sb("w1_hi", [P, NF, H], F32R)
        w1_lo = sb("w1_lo", [P, NF, H], F32R)
        w2 = sb("w2", [P, NF, H])
        w0 = sb("w0", [ROWS0, CHUNKS0, H])
        w0_mirror = sb("w0_mirror", [ROWS0, CHUNKS0, H])
        pick_raw = sb("pick_raw", [SELK, CHUNKS0, ROWS0])
        pick = sb("pick", [SELK, CHUNKS0, ROWS0], F32R)
        ident = sb("ident", [P, P])
        own_row = sb("own_row", [P, TILE])
        bias0 = sb("bias0", [P, 1])
        bias1 = sb("bias1", [P, H])
        bias2 = sb("bias2", [P, 1])
        bias2_sum = sb("bias2_sum", [P, 1])
        wt1 = sb("wt1", [P, 3, 512])
        wt1_dense = sb("wt1_dense", [D, 512])
        wt2 = sb("wt2", [P, 4, 256])
        wt3 = sb("wt3", [P, 2])
        bt1 = sb("bt1", [P, 4])
        bt2 = sb("bt2", [P, 2])
        ids = sb("ids", [P, NF], I32)
        gathered = sb("gathered", [P, NF, D])
        e_rows = sb("e_rows", [P, D, ROWS0])
        x0 = sb("x0", [ROWS0, COLS])
        x0_split = sb("x0_split", [SELK, COLS], F32R)
        x0_t = [sb(f"x0_t{i}", [P, TILES, NF]) for i in range(2)]
        x0_blocks = [sb(f"x0_blocks{i}", [P, TILES, NP2, TILE]) for i in range(2)]
        prods = [sb(f"prods{i}", [ROWS0, COLS]) for i in range(2)]
        x1 = sb("x1", [P, COLS])
        x1_hi = [sb(f"x1_hi{i}", [P, COLS], F32R) for i in range(2)]
        x1_lo = [sb(f"x1_lo{i}", [P, COLS], F32R) for i in range(2)]
        terms = [[sb(f"terms{i}{q}", [P, TERMS + 1, H]) for q in range(2)] for i in range(2)]
        pair_sums = sb("pair_sums", [P, NP2, GROUP])
        w1_raw = pair_sums
        z0 = sb("z0", [P, GROUP])
        z_top = sb("z_top", [P, 3, GROUP])
        dense = sb("dense", [D, GROUP])
        h1 = sb("h1", [P, 4, GROUP])
        h2 = sb("h2", [P, 2, GROUP])
        y = sb("y", [1, GROUP])

        part = [[ps(f"part{i}{q}", [P, 512]) for q in range(2)] for i in range(2)]
        ps_pick = ps("ps_pick", [P, 512])
        ps_x1 = ps("ps_x1", [P, 512])
        ps_misc = ps("ps_misc", [P, 512])
        ps_top = ps("ps_top", [P, 512])

        s_w1 = sem("w1_loaded")
        s_w0 = sem("w0_loaded")
        s_const = sem("constants_loaded")
        s_top_w = sem("top_weights_loaded")
        s_ids = sem("ids_loaded")
        s_gathered = sem("tables_gathered")
        s_zeroed = sem("x0_split_zeroed")
        s_w1hi = sem("w1_hi_ready")
        s_w1lo = sem("w1_lo_ready")
        s_w0sum = sem("w0_folded")
        s_pick_r = sem("pick_ready")
        s_b2 = sem("bias2_sum_ready")
        s_ones = sem("own_row_columns_ready")
        s_erows = sem("e_rows_ready")
        s_turned = sem("x0_turned")
        s_x0 = sem("x0_ready")
        s_x0hi = sem("x0_hi_ready")
        s_x0lo = sem("x0_lo_ready")
        s_turned_t = sem("x0_t_turned")
        s_x0t = sem("x0_t_ready")
        s_blocks = sem("x0_blocks_ready")
        s_picked = sem("x0_picked")
        s_prods = sem("products_ready")
        s_l0 = sem("layer0_matmuls")
        s_x1 = sem("x1_ready")
        s_x1hi = sem("x1_hi_ready")
        s_x1lo = sem("x1_lo_ready")
        s_z0 = sem("z0_ready")
        s_part = sem("part_full")
        s_acc = sem("vector_terms_added")
        s_term = sem("scalar_terms_ready")
        s_tree = sem("gpsimd_sums")
        s_x2 = sem("x2_ready")
        s_p2 = sem("pair_sums_done")
        s_p2out = sem("pair_sums_stored")
        s_ztop = sem("z_top_copies")
        s_z2 = sem("z2_done")
        s_z2out = sem("z2_stored")
        s_dense = sem("dense_loaded")
        s_h1 = sem("h1_done")
        s_h1out = sem("h1_stored")
        s_h2 = sem("h2_done")
        s_h2out = sem("h2_stored")
        s_y = sem("y_done")
        s_yout = sem("y_copied")
        s_stored = sem("y_written")

        s_met = sem("transposes_begun")
        s_begun = sem("gathers_begun")

        def some(count):
            return not isinstance(count, int) or count > 0

        def tile(q, n):
            return slice((2 * n + q) * P, (2 * n + q + 1) * P)

        block = ctx.enter_context(nc.Block())

        @block.sync
        def _(sp):
            sp.dma_start(ids[:], t["ids"][0:GROUP, :]).then_inc(s_ids, 16)
            sp.dma_start(ident[:], t["ident"]).then_inc(s_const, 16)
            sp.dma_start(own_row[:], t["own_row"]).then_inc(s_const, 16)
            sp.dma_start(pick_raw[:], t["pick"]).then_inc(s_const, 16)
            sp.dma_start(bias0[:], t["b0"]).then_inc(s_const, 16)
            sp.dma_start(bias1[:], t["b1"].to_broadcast([P, H])).then_inc(s_const, 16)
            sp.dma_start(bias2[:], t["b2"]).then_inc(s_const, 16)
            sp.dma_start(w1_raw[:, 0:NF, :], t["w1"]).then_inc(s_w1, 16)
            sp.dma_start(w0[:], t["w0"]).then_inc(s_w0, 16)
            sp.dma_start(w0_mirror[:], t["w0_mirror"]).then_inc(s_w0, 16)
            sp.dma_start(w2[:], t["w2"]).then_inc(s_top_w, 16)
            sp.dma_start(wt1[:], t["wt1"]).then_inc(s_top_w, 16)
            sp.dma_start(wt1_dense[:], t["wt1_dense"]).then_inc(s_top_w, 16)
            sp.dma_start(wt2[:], t["wt2"]).then_inc(s_top_w, 16)
            sp.dma_start(wt3[:], t["wt3"]).then_inc(s_top_w, 16)
            sp.dma_start(bt1[:], t["bt1"]).then_inc(s_top_w, 16)
            sp.dma_start(bt2[:], t["bt2"]).then_inc(s_top_w, 16)

            def group(g, first, last):
                if not last:
                    sp.wait_ge(s_gathered, (g + 1) * NF * 16)
                    sp.dma_start(ids[:], t["ids"][bass.ds((g + 1) * GROUP, GROUP), :]).then_inc(s_ids, 16)
                if not first:
                    sp.wait_ge(s_h1, g)
                sp.dma_start(dense[:], t["dense"][:, bass.ds(g * GROUP, GROUP)]).then_inc(s_dense, 16)
                if not first:
                    sp.wait_ge(s_yout, g)
                    sp.dma_start(t["y"][:, bass.ds((g - 1) * GROUP, GROUP)], y[:]).then_inc(s_stored, 16)

            group(0, True, False)
            with sp.Fori(1, GROUPS - 1) as g:
                group(g, False, False)
            group(GROUPS - 1, False, True)
            sp.wait_ge(s_yout, GROUPS)
            sp.dma_start(t["y"][:, B - GROUP:B], y[:]).then_inc(s_stored, 16)
            sp.wait_ge(s_stored, 16 * GROUPS)

        @block.gpsimd
        def _(pool):
            def gather(fields):
                for f in fields:
                    pool.indirect_dma_start(
                        out=gathered[:, f, :], out_offset=None, in_=t[f"tbl_{f}"],
                        in_offset=bass.IndirectOffsetOnAxis(ap=ids[:, f:f + 1].bitcast(U32), axis=0),
                    ).then_inc(s_gathered, 16)

            def spread(par, m):
                pool.wait_ge(s_x0t, m + 1)
                if some(TILES * (m - 1)):
                    pool.wait_ge(s_p2, TILES * (m - 1))
                for i in range(TILES):
                    ins = pool.tensor_tensor(
                        x0_blocks[par][:, i, 0:NF, :],
                        x0_t[par][:, i, :].unsqueeze(2).to_broadcast([P, NF, TILE]),
                        own_row[:].unsqueeze(1).to_broadcast([P, NF, TILE]), ALU.mult)
                ins.then_inc(s_blocks, 1)

            def sums(u, i):
                k = 6 * u
                for q, x in enumerate(terms[i]):
                    pool.wait_ge(s_term, 2 * TERMS * u + ACT_UPTO[ACT_CHUNKS[-1] + 1] - 4 * (1 - q))
                    pool.tensor_tensor(x[:, 0:4, :], x[:, 0:4, :], x[:, 4:8, :], ALU.add).then_inc(s_tree, 1)
                for q, x in enumerate(terms[i]):
                    pool.wait_ge(s_tree, k + 1 + q)
                    pool.tensor_tensor(x[:, 0:2, :], x[:, 0:2, :], x[:, 2:4, :], ALU.add).then_inc(s_tree, 1)
                for q, x in enumerate(terms[i]):
                    pool.wait_ge(s_tree, k + 3 + q)
                    pool.tensor_tensor(x[:, 0, :], x[:, 0, :], x[:, 1, :], ALU.add).then_inc(s_tree, 1)
                for q, x in enumerate(terms[i]):
                    pool.wait_ge(s_acc, PER_PAIR * (u + 1) - 1 + q)
                    pool.wait_ge(s_tree, k + 5 + q)
                    pool.tensor_tensor(x[:, 0, :], x[:, 0, :], x[:, TERMS, :], ALU.add).then_inc(s_x2, 1)

            pool.memset(x0_split[:].bitcast(F32), 0.0).then_inc(s_zeroed, 1)
            pool.wait_ge(s_ids, 16)
            gather(range(NF))
            pool.wait_ge(s_const, 16 * 6)
            for par in range(2):
                for i in range(TILES):
                    pool.tensor_copy(x0_blocks[par][:, i, NF, :], own_row[:]).then_inc(s_ones, 1)
            spread(0, 0)

            def group(g, last):
                for blk in range(BLOCKS):
                    n = BLOCKS * g + blk
                    if not (last and blk == BLOCKS - 1):
                        spread((blk + 1) % 2, n + 1)
                    for p in range(PAIRS):
                        i = PAIRS * blk + p
                        if not last and i * GATHERS < NF:
                            if i == 0:
                                pool.wait_ge(s_ids, 16 * (g + 2))
                                pool.wait_ge(s_erows, g + 1)
                                pool.sem_inc(s_begun, 1)
                            gather(range(i * GATHERS, min(NF, (i + 1) * GATHERS)))
                        sums(PAIRS * n + p, p)

            group(0, False)
            with pool.Fori(1, GROUPS - 1) as g:
                group(g, False)
            group(GROUPS - 1, True)

        @block.scalar
        def _(act):
            def erows(g):
                act.wait_ge(s_gathered, (g + 1) * NF * 16)
                if some(BLOCKS * g):
                    act.wait_ge(s_turned, BLOCKS * g)
                act.activation(e_rows[:].rearrange("p d (r j) -> p d r j", r=3),
                               gathered[:].rearrange("p j d -> p d j").unsqueeze(2).to_broadcast([P, D, 3, NF]),
                               ACT.Copy).then_inc(s_erows, 1)

            def store_x0(m):
                act.wait_ge(s_turned, m + 1)
                if some(m):
                    act.wait_ge(s_x0lo, m)
                if some(CHUNKS0 * m):
                    act.wait_ge(s_prods, CHUNKS0 * m)
                src = ps_misc[0:ROWS0, :].rearrange("p (d b) -> p b d", d=D)
                act.activation(x0[:].rearrange("p (b d) -> p b d", d=D), src, ACT.Copy).then_inc(s_x0, 1)
                act.activation(x0_split[0:NF, :].rearrange("p (b d) -> p b d", d=D), src[0:NF],
                               ACT.Copy).then_inc(s_x0hi, 1)

            def store_x0t(par, m):
                act.wait_ge(s_turned_t, m + 1)
                act.activation(x0_t[par][:].rearrange("p i j -> p (i j)"), ps_misc[:, 0:TILES * NF],
                               ACT.Copy).then_inc(s_x0t, 1)

            def store_x1(par, m):
                act.wait_ge(s_l0, CHUNKS0 * (m + 1))
                if some(m):
                    act.wait_ge(s_z0, m)
                act.activation(x1_hi[par][:], ps_x1[:], ACT.Identity, bias=bias0[:]).then_inc(s_x1hi, 1)
                act.activation(x1[:], ps_x1[:], ACT.Identity, bias=bias0[:]).then_inc(s_x1, 1)

            def store_pair_sums(i, col):
                act.wait_ge(s_p2, i + 1)
                act.activation(pair_sums[:, :, bass.ds(col, TILE)],
                               ps_misc[:, 0:NP2 * TILE].rearrange("p (j b) -> p j b", b=TILE),
                               ACT.Copy).then_inc(s_p2out, 1)

            def multiply(v, c, p, par):
                for q in range(2):
                    act.wait_ge(s_part, 2 * v + 1 + q)
                    for n, j in enumerate(FIELDS[c]):
                        act.activation(terms[p][q][:, ACT_UPTO[c] // 2 + n, :], part[c % 2][q][:, n * H:(n + 1) * H],
                                       ACT.Copy, scale=x0_t[par][:, 2 * p + q, j:j + 1]).then_inc(s_term, 1)

            def store_z1(g):
                act.wait_ge(s_p2out, (g + 1) * GROUP // TILE)
                act.activation(z_top[:, 1, :], pair_sums[:, NF, :], ACT.Copy).then_inc(s_ztop, 1)

            def store_z2(g):
                act.wait_ge(s_z2, g + 1)
                act.activation(z_top[:, 2, :], ps_top[:, 0:GROUP], ACT.Identity,
                               bias=bias2_sum[:]).then_inc(s_z2out, 1)

            def store_h1(g):
                act.wait_ge(s_h1, g + 1)
                for i in range(4):
                    act.activation(h1[:, i, :], ps_top[:, i * GROUP:(i + 1) * GROUP], ACT.Relu,
                                   bias=bt1[:, i:i + 1]).then_inc(s_h1out, 1)

            def store_h2(g):
                act.wait_ge(s_h2, g + 1)
                for i in range(2):
                    act.activation(h2[:, i, :], ps_top[:, i * GROUP:(i + 1) * GROUP], ACT.Relu,
                                   bias=bt2[:, i:i + 1]).then_inc(s_h2out, 1)

            def store_y(g):
                act.wait_ge(s_y, g + 1)
                if some(16 * g):
                    act.wait_ge(s_stored, 16 * g)
                act.activation(y[:], ps_top[0:1, 0:GROUP], ACT.Copy).then_inc(s_yout, 1)

            act.wait_ge(s_const, 16 * 6)
            act.activation(pick[:], pick_raw[:], ACT.Copy).then_inc(s_pick_r, 1)
            act.mul(bias2_sum[:], bias2[:], float(D)).then_inc(s_b2, 1)
            act.wait_ge(s_b2, 1)
            act.wait_ge(s_w1, 16)
            act.activation(w1_hi[:], w1_raw[:, 0:NF, :], ACT.Copy).then_inc(s_w1hi, 1)
            erows(0)
            act.wait_ge(s_zeroed, 1)
            store_x0(0)
            store_x0t(0, 0)
            store_x1(0, 0)

            def group(g, first, last):
                for blk in range(BLOCKS):
                    n = BLOCKS * g + blk
                    more = not (last and blk == BLOCKS - 1)
                    for s in range(STEPS):
                        p, c = divmod(s, CHUNKS)
                        if c in ACT_CHUNKS:
                            multiply(STEPS * n + s, c, p, blk % 2)
                        if s == 0 and more:
                            store_x0(n + 1)
                        if s in (3, 4) and not (first and blk == 0):
                            col = (BLOCK * blk - BLOCK + (s - 1) * TILE) % GROUP
                            store_pair_sums(TILES * n - 5 + s, col)
                        if s == 5 and more:
                            store_x0t((blk + 1) % 2, n + 1)
                        if s == 5 and blk == 0 and not first:
                            store_z1(g - 1)
                        if s == 16 and more:
                            store_x1((blk + 1) % 2, n + 1)
                        if s in (17, 18):
                            store_pair_sums(TILES * n + s - 17, BLOCK * blk + (s - 17) * TILE)
                        if s == 10 and blk == 2 and not last:
                            erows(g + 1)
                        if s == 6 and blk == 3:
                            act.wait_ge(s_z0, n + 1)
                            if not first:
                                act.wait_ge(s_h1, g)
                            act.activation(z_top[:, 0, :], z0[:], ACT.Copy).then_inc(s_ztop, 1)
                        if not first:
                            if blk == 0 and s == 16:
                                store_z2(g - 1)
                            if blk == 1 and s == 11:
                                store_h1(g - 1)
                            if blk == 2 and s == 11:
                                store_h2(g - 1)
                            if blk == 3 and s == 8:
                                store_y(g - 1)

            group(0, True, False)
            with act.Fori(1, GROUPS - 1) as g:
                group(g, False, False)
            group(GROUPS - 1, False, True)
            for q in range(2):
                store_pair_sums(B // TILE - 2 + q, GROUP - (2 - q) * TILE)
            store_z1(GROUPS - 1)
            store_z2(GROUPS - 1)
            store_h1(GROUPS - 1)
            store_h2(GROUPS - 1)
            store_y(GROUPS - 1)

        @block.vector
        def _(dve):
            def split_x0(m):
                dve.wait_ge(s_x0, m + 1)
                dve.wait_ge(s_x0hi, m + 1)
                dve.tensor_tensor(x0_split[LO:LO + NF, :], x0[0:NF, :], x0_split[0:NF, :].bitcast(F32),
                                  ALU.subtract).then_inc(s_x0lo, 1)

            def product(m, c):
                k = CHUNKS0 * m + c
                dve.wait_ge(s_picked, k + 1)
                if some(k - 1):
                    dve.wait_ge(s_l0, k - 1)
                r = rows0(c)
                dve.tensor_tensor(prods[c % 2][0:r, :], ps_pick[0:r, :], x0[0:r, :], ALU.mult).then_inc(s_prods, 1)

            def split_x1(par, m):
                dve.wait_ge(s_x1, m + 1)
                dve.wait_ge(s_x1hi, m + 1)
                dve.tensor_tensor(x1_lo[par][:], x1[:], x1_hi[par][:].bitcast(F32),
                                  ALU.subtract).then_inc(s_x1lo, 1)

            def sum_x1(m, col):
                dve.tensor_reduce(z0[:, bass.ds(col, BLOCK)], x1[:].rearrange("p (b d) -> p b d", d=D),
                                  AX.X, ALU.add).then_inc(s_z0, 1)

            def add_terms(u, c, p, par):
                k = PER_PAIR * u + DVE_UPTO[c]
                for n, j in enumerate(FIELDS[c]):
                    for q in range(2):
                        if n == 0:
                            dve.wait_ge(s_part, 2 * (CHUNKS * u + c) + 1 + q)
                        if c or n:
                            dve.wait_ge(s_acc, k + 2 * n + q - 1)
                        total = terms[p][q][:, TERMS, :]
                        dve.scalar_tensor_tensor(
                            out=total, in0=part[c % 2][q][:, n * H:(n + 1) * H],
                            scalar=x0_t[par][:, 2 * p + q, j:j + 1], in1=total if c or n else bias1[:],
                            op0=ALU.mult, op1=ALU.add).then_inc(s_acc, 1)

            dve.wait_ge(s_w0, 32)
            dve.tensor_tensor(w0[:], w0[:], w0_mirror[:], ALU.add).then_inc(s_w0sum, 1)
            dve.wait_ge(s_w1hi, 1)
            dve.tensor_tensor(w1_lo[:], w1_raw[:, 0:NF, :], w1_hi[:].bitcast(F32), ALU.subtract).then_inc(s_w1lo, 1)
            dve.wait_ge(s_zeroed, 1)
            split_x0(0)
            for c in range(CHUNKS0):
                product(0, c)
            split_x1(0, 0)
            sum_x1(0, 0)
            dve.wait_ge(s_const, 16 * 6)
            dve.wait_ge(s_x0t, 1)

            def group(g, last):
                for blk in range(BLOCKS):
                    n = BLOCKS * g + blk
                    more = not (last and blk == BLOCKS - 1)
                    for s in range(STEPS):
                        p, c = divmod(s, CHUNKS)
                        if c not in ACT_CHUNKS:
                            add_terms(PAIRS * n + p, c, p, blk % 2)
                        if not more:
                            continue
                        if s == 1:
                            split_x0(n + 1)
                        if s in range(2, 2 + 2 * CHUNKS0, 2):
                            product(n + 1, s // 2 - 1)
                        if s == 17:
                            split_x1((blk + 1) % 2, n + 1)
                        if s == 18:
                            if blk == BLOCKS - 1:
                                dve.wait_ge(s_ztop, 2 * g + 1)
                            sum_x1(n + 1, BLOCK * ((blk + 1) % BLOCKS))

            group(0, False)
            with dve.Fori(1, GROUPS - 1) as g:
                group(g, False)
            group(GROUPS - 1, True)

        @block.tensor
        def _(pe):
            def turn_x0(blk, m):
                pe.wait_ge(s_erows, m // BLOCKS + 1 if isinstance(m, int) else erow_count[0])
                if some(m):
                    pe.wait_ge(s_x0t, m)
                if some(TILES * (m - 1) - 2):
                    pe.wait_ge(s_p2out, TILES * (m - 1) - 2)
                pe.sem_inc(s_met, 1)
                r = slice(BLOCK * blk, BLOCK * (blk + 1))
                for d in range(D):
                    ins = pe.transpose(ps_misc[0:ROWS0, d * BLOCK:(d + 1) * BLOCK], e_rows[r, d, :], ident[r, r])
                ins.then_inc(s_turned, 1)

            def turn_x0t(m):
                pe.wait_ge(s_x0, m + 1)
                pe.wait_ge(s_x0hi, m + 1)
                if some(TILES * (m - 1)):
                    pe.wait_ge(s_p2out, TILES * (m - 1))
                pe.sem_inc(s_met, 1)
                for i in range(TILES):
                    ins = pe.transpose(ps_misc[:, i * NF:(i + 1) * NF], x0[0:NF, i * P:(i + 1) * P],
                                       ident[0:NF, 0:NF])
                ins.then_inc(s_turned_t, 1)

            def pick_rows(m, c):
                if some(CHUNKS0 * m + c):
                    pe.wait_ge(s_prods, CHUNKS0 * m + c)
                r = rows0(c)
                pe.matmul(ps_pick[0:r, :], pick[:, c, 0:r], x0_split[:, :], start=True,
                          stop=True).then_inc(s_picked, 1)

            def layer0(m, c):
                pe.wait_ge(s_prods, CHUNKS0 * m + c + 1)
                if c == 0:
                    if some(m):
                        pe.wait_ge(s_x1, m)
                r = rows0(c)
                pe.matmul(ps_x1[:], w0[0:r, c, :], prods[c % 2][0:r, :], start=(c == 0),
                          stop=(c == CHUNKS0 - 1)).then_inc(s_l0, 1)

            def layer1(u, c, p, par):
                w = len(FIELDS[c]) * H
                f = slice(FIELDS[c][0], FIELDS[c][-1] + 1)
                c2, u2 = (c - 2) % CHUNKS, u - (c < 2)
                for q in range(2):
                    if c2 in ACT_CHUNKS:
                        if some(2 * TERMS * u2 + ACT_UPTO[c2 + 1] - 4 * (1 - q)):
                            pe.wait_ge(s_term, 2 * TERMS * u2 + ACT_UPTO[c2 + 1] - 4 * (1 - q))
                    else:
                        if some(PER_PAIR * u2 + DVE_UPTO[c2 + 1] - 1 + q):
                            pe.wait_ge(s_acc, PER_PAIR * u2 + DVE_UPTO[c2 + 1] - 1 + q)
                    out = part[c % 2][q][:, 0:w]
                    hi = x1_hi[par][:, tile(q, p)]
                    lo = x1_lo[par][:, tile(q, p)]
                    pe.matmul(out, hi, w1_hi[:, f, :], start=True, stop=False)
                    pe.matmul(out, hi, w1_lo[:, f, :], start=False, stop=False)
                    if c == 0 and p == 0 and q == 0:
                        pe.wait_ge(s_x1lo, u // PAIRS + 1 if isinstance(u, int) else block_count[0])
                    pe.matmul(out, lo, w1_hi[:, f, :], start=False, stop=True).then_inc(s_part, 1)

            def sum_pairs(i, par, k, p, q, m):
                pe.wait_ge(s_x2, i + 1)
                if some(i):
                    pe.wait_ge(s_p2out, i)
                pe.matmul(ps_misc[:, 0:NP2 * TILE], terms[p][q][:, 0, :],
                          x0_blocks[par][:, k, :, :].rearrange("p j b -> p (j b)"), start=True,
                          stop=True).then_inc(s_p2, 1)

            def z2(g, js):
                if js[0] == 0:
                    pe.wait_ge(s_p2out, (g + 1) * GROUP // TILE)
                    if some(g):
                        pe.wait_ge(s_yout, g)
                for j in js:
                    ins = pe.matmul(ps_top[:, 0:GROUP], w2[:, j, :], pair_sums[:, j, :], start=(j == 0),
                                    stop=(j == NF - 1))
                if js[-1] == NF - 1:
                    ins.then_inc(s_z2, 1)

            def top1(g, i, last):
                if i == 0:
                    pe.wait_ge(s_z2out, g + 1)
                    pe.wait_ge(s_ztop, 2 * g + 2)
                    pe.wait_ge(s_dense, 16 * (g + 1))
                out = ps_top[:, i * GROUP:(i + 1) * GROUP]
                for k in range(3):
                    pe.matmul(out, wt1[:, k, i * P:(i + 1) * P], z_top[:, k, :], start=(k == 0), stop=False)
                ins = pe.matmul(out, wt1_dense[:, i * P:(i + 1) * P], dense[:], start=False, stop=True)
                if i == 3:
                    ins.then_inc(s_h1, 1)

            def top2(g, i):
                if i == 0:
                    pe.wait_ge(s_h1out, 4 * (g + 1))
                for k in range(4):
                    ins = pe.matmul(ps_top[:, i * GROUP:(i + 1) * GROUP], wt2[:, k, i * P:(i + 1) * P],
                                    h1[:, k, :], start=(k == 0), stop=(k == 3))
                if i == 1:
                    ins.then_inc(s_h2, 1)

            def top3(g):
                pe.wait_ge(s_h2out, 2 * (g + 1))
                for k in range(2):
                    ins = pe.matmul(ps_top[0:1, 0:GROUP], wt3[:, k:k + 1], h2[:, k, :], start=(k == 0),
                                    stop=(k == 1))
                ins.then_inc(s_y, 1)

            erow_count = [1]
            block_count = [1]
            pe.wait_ge(s_const, 16 * 6)
            turn_x0(0, 0)
            turn_x0t(0)
            pe.wait_ge(s_pick_r, 1)
            pe.wait_ge(s_x0lo, 1)
            pe.wait_ge(s_w0sum, 1)
            for c in range(CHUNKS0):
                pick_rows(0, c)
                layer0(0, c)
            pe.wait_ge(s_x1hi, 1)
            pe.wait_ge(s_w1lo, 1)
            pe.wait_ge(s_top_w, 16 * 7)

            Z2_STEP = 4

            def group(g, first, last):
                for blk in range(BLOCKS):
                    n = BLOCKS * g + blk
                    more = not (last and blk == BLOCKS - 1)
                    par, nxt = blk % 2, (blk + 1) % 2
                    erow_count[0] = g + 1 + (blk + 1) // BLOCKS
                    block_count[0] = n + 1
                    for s in range(STEPS):
                        p, c = divmod(s, CHUNKS)
                        layer1(PAIRS * n + p, c, p, par)
                        if s == 0 and more:
                            turn_x0((blk + 1) % BLOCKS, n + 1)
                        if s == 2 and more:
                            pe.wait_ge(s_x0lo, n + 2)
                        if s in range(2, 2 + 2 * CHUNKS0, 2) and more:
                            pick_rows(n + 1, s // 2 - 1)
                        if s in range(4, 4 + 2 * CHUNKS0, 2) and more:
                            layer0(n + 1, s // 2 - 2)
                        if s in (3, 4) and not (first and blk == 0):
                            if s == 3 and more:
                                pe.wait_ge(s_x0, n + 2)
                                pe.wait_ge(s_x0hi, n + 2)
                            sum_pairs(TILES * n - 5 + s, nxt, s - 1, 1, s - 3, n - 1)
                        if s == 5 and more:
                            turn_x0t(n + 1)
                        if s in (17, 18):
                            if s == 17:
                                pe.wait_ge(s_blocks, n + 1)
                                if more:
                                    pe.wait_ge(s_x0t, n + 2)
                            sum_pairs(TILES * n + s - 17, par, s - 17, 0, s - 17, n)
                        if not first:
                            if blk == 0 and 6 <= s < 16:
                                z2(g - 1, range((s - 6) * Z2_STEP, min(NF, (s - 5) * Z2_STEP)))
                            if blk == 1 and s in (3, 5, 7, 9):
                                top1(g - 1, (s - 3) // 2, last)
                            if blk == 2 and s in (5, 7):
                                top2(g - 1, (s - 5) // 2)
                            if blk == 3 and s == 5:
                                top3(g - 1)
                    if more:
                        pe.wait_ge(s_x1hi, n + 2)

            group(0, True, False)
            with pe.Fori(1, GROUPS - 1) as g:
                group(g, False, False)
            group(GROUPS - 1, False, True)
            g = GROUPS - 1
            for q in range(2):
                sum_pairs(B // TILE - 2 + q, 1, 2 + q, 1, q, 0)
            z2(g, range(NF))
            for i in range(4):
                top1(g, i, True)
            for i in range(2):
                top2(g, i)
            top3(g)


def kernel(**inputs):
    import concourse.bacc as bacc
    from concourse.bass_utils import run_bass_kernel_spmd as run

    x = {k: np.asarray(v) for k, v in inputs.items()}
    first = np.tile(np.arange(NF), 3 * CHUNKS0)
    shift = np.repeat(np.arange(3 * CHUNKS0), NF)
    second = (first + shift) % NF
    W0 = x["L0_rec_W0"].reshape(H, NF, NF)
    used = (shift < SHIFTS)[:, None]
    w0 = np.where(used, W0[:, first, second].T, np.float32(0))
    mirror = np.where(used & (shift > 0)[:, None], W0[:, second, first].T, np.float32(0))

    def chunks0(a):
        return a.reshape(CHUNKS0, ROWS0, H).transpose(1, 0, 2)

    pick = np.zeros((SELK, CHUNKS0 * ROWS0), np.float32)
    cols = np.arange(CHUNKS0 * ROWS0)
    pick[second, cols] = 1
    pick[LO + second, cols] = 1
    arrays = {
        "ids": x["ids"],
        "dense": x["dense_ctx"].T,
        "ident": np.eye(P, dtype=np.float32),
        "own_row": np.repeat(np.eye(TILE, dtype=np.float32), D, axis=0),
        "pick": pick.reshape(SELK, CHUNKS0, ROWS0),
        "w0": chunks0(w0),
        "w0_mirror": chunks0(mirror),
        "w1": x["L0_rec_W1"].reshape(H, NF, H).transpose(2, 1, 0),
        "w2": x["L0_rec_W2"].reshape(H, NF, H).transpose(2, 1, 0),
        "b0": x["L0_rec_b0"].reshape(H, 1),
        "b1": x["L0_rec_b1"].reshape(1, H),
        "b2": x["L0_rec_b2"].reshape(H, 1),
        "wt1": x["W_top1"][:3 * P].reshape(3, P, 512).transpose(1, 0, 2),
        "wt1_dense": x["W_top1"][3 * P:],
        "wt2": x["W_top2"].reshape(4, P, 256).transpose(1, 0, 2),
        "wt3": x["W_top3"].reshape(2, P).T,
        "bt1": x["b_top1"].reshape(4, P).T,
        "bt2": x["b_top2"].reshape(2, P).T,
    }
    arrays.update({f"tbl_{f}": x[f"tbl_{f}"] for f in range(NF)})
    nc = bacc.Bacc("TRN2", target_bir_lowering=False, num_devices=1)
    given, t = {}, {}
    for name, a in arrays.items():
        a = np.ascontiguousarray(a)
        given[f"in_{name}"] = a
        t[name] = nc.dram_tensor(f"in_{name}", a.shape, mybir.dt.from_np(a.dtype), kind="ExternalInput").ap()
    t["y"] = nc.dram_tensor("out_y", (1, B), F32, kind="ExternalOutput").ap()
    build(nc, t)
    r = run(nc, [given], core_ids=[0])
    return r.results[0]["out_y"].reshape(B, 1)
```

```python
from contextlib import ExitStack

import numpy as np
import concourse.bass as bass
from concourse import mybir

F32 = mybir.dt.float32
F32R = mybir.dt.float32r
I32 = mybir.dt.int32
U32 = mybir.dt.uint32
ALU = mybir.AluOpType
ACT = mybir.ActivationFunctionType
AX = mybir.AxisListType

P = 128
NF = 39
D = 16
H = 128
B = 1024
GROUP = 128
GROUPS = B // GROUP
BLOCK = 32
BLOCKS = GROUP // BLOCK
COLS = BLOCK * D
TILE = P // D
TILES = BLOCK // TILE
PAIRS = TILES // 2
CHUNKS = 10
STEPS = PAIRS * CHUNKS
SHIFTS = NF // 2 + 1
ROWS0 = 3 * NF
CHUNKS0 = -(-SHIFTS // 3)
NP2 = NF + 1

FIELDS = [range(4 * c, min(4 * c + 4, NF)) for c in range(CHUNKS)]
ACT_CHUNKS = (1, 3, 5, 7, 9)
TERMS = sum(len(FIELDS[c]) for c in ACT_CHUNKS)
DVE_UPTO, ACT_UPTO = [0], [0]
for c, f in enumerate(FIELDS):
    DVE_UPTO.append(DVE_UPTO[-1] + 2 * len(f) * (c not in ACT_CHUNKS))
    ACT_UPTO.append(ACT_UPTO[-1] + 2 * len(f) * (c in ACT_CHUNKS))
PER_PAIR = DVE_UPTO[-1]
PRODUCTS_AT = {2: [0], 6: [1, 2], 8: [3, 4], 12: [5, 6]}
LAYER0_AT = {5: [0], 8: [1], 9: [2], 11: [3], 12: [4], 15: [5], 16: [6]}
PROD_BUFS = 3
TOP1_AT = [2, 4, 6, 13]
PARTS = 5
GATHERS = 8


def shifts0(c):
    return range(3 * c, min(3 * c + 3, SHIFTS))


def bank(c, q):
    return (2 * c + q) % PARTS


def rows0(c):
    return NF * len(shifts0(c))


def build(nc, t):
    ctx = ExitStack()
    with ctx:
        def sb(name, shape, dt=F32):
            return ctx.enter_context(nc.sbuf_tensor(name, shape, dt))

        def ps(name, shape):
            return ctx.enter_context(nc.psum_tensor(name, shape, F32))

        def sem(name):
            return ctx.enter_context(nc.semaphore(name))

        w1_hi = sb("w1_hi", [P, NF, H], F32R)
        w1_lo = sb("w1_lo", [P, NF, H], F32R)
        w2 = sb("w2", [P, NF, H])
        w0 = sb("w0", [ROWS0, CHUNKS0, H])
        w0_mirror = sb("w0_mirror", [ROWS0, CHUNKS0, H])
        ident = sb("ident", [P, P])
        own_row = sb("own_row", [P, TILE])
        bias0 = sb("bias0", [P, 1])
        bias1 = sb("bias1", [P, H])
        bias2 = sb("bias2", [P, 1])
        bias2_sum = sb("bias2_sum", [P, 1])
        wt1 = sb("wt1", [P, 3, 512])
        wt1_dense = sb("wt1_dense", [D, 512])
        wt2 = sb("wt2", [P, 4, 256])
        wt3 = sb("wt3", [P, 2])
        bt1 = sb("bt1", [P, 4])
        bt2 = sb("bt2", [P, 2])
        ids = sb("ids", [P, NF], I32)
        gathered = sb("gathered", [P, NF, D])
        e_rows = sb("e_rows", [P, D, ROWS0])
        x0 = sb("x0", [ROWS0, COLS])
        x0_shifted = sb("x0_shifted", [ROWS0, CHUNKS0, COLS])
        x0_t = [sb(f"x0_t{i}", [P, TILES, NF]) for i in range(2)]
        x0_blocks = [sb(f"x0_blocks{i}", [P, TILES, NP2, TILE]) for i in range(2)]
        prods = [sb(f"prods{i}", [ROWS0, COLS]) for i in range(PROD_BUFS)]
        x1 = sb("x1", [P, COLS])
        x1_hi = [sb(f"x1_hi{i}", [P, COLS], F32R) for i in range(2)]
        x1_lo = [sb(f"x1_lo{i}", [P, COLS], F32R) for i in range(2)]
        terms = [[sb(f"terms{i}{q}", [P, TERMS + 1, H]) for q in range(2)] for i in range(2)]
        pair_sums = sb("pair_sums", [P, NP2, GROUP])
        w1_raw = pair_sums
        z0 = sb("z0", [P, GROUP])
        z_top = sb("z_top", [P, 3, GROUP])
        dense = sb("dense", [D, GROUP])
        h1 = sb("h1", [P, 4, GROUP])
        h2 = sb("h2", [P, 2, GROUP])
        y = sb("y", [1, GROUP])

        parts = [ps(f"part{i}", [P, 512]) for i in range(PARTS)]
        ps_x1 = ps("ps_x1", [P, 512])
        ps_misc = ps("ps_misc", [P, 512])
        ps_top = ps("ps_top", [P, 512])

        s_w1 = sem("w1_loaded")
        s_w0 = sem("w0_loaded")
        s_const = sem("constants_loaded")
        s_top_w = sem("top_weights_loaded")
        s_ids = sem("ids_loaded")
        s_gathered = sem("tables_gathered")
        s_w1hi = sem("w1_hi_ready")
        s_w1lo = sem("w1_lo_ready")
        s_w0sum = sem("w0_folded")
        s_b2 = sem("bias2_sum_ready")
        s_ones = sem("own_row_columns_ready")
        s_erows = sem("e_rows_ready")
        s_turned = sem("x0_turned")
        s_x0 = sem("x0_ready")
        s_turned_t = sem("x0_t_turned")
        s_x0t = sem("x0_t_ready")
        s_blocks = sem("x0_blocks_ready")
        s_shifted = [sem(f"x0_shifted{c}_loaded") for c in range(CHUNKS0)]
        s_prods = sem("products_ready")
        s_l0 = sem("layer0_matmuls")
        s_x1 = sem("x1_ready")
        s_x1hi = sem("x1_hi_ready")
        s_x1lo = sem("x1_lo_ready")
        s_z0 = sem("z0_ready")
        s_part = sem("part_full")
        s_acc = sem("vector_terms_added")
        s_term = sem("scalar_terms_ready")
        s_tree = sem("gpsimd_sums")
        s_folds = sem("vector_folds")
        s_x2 = sem("x2_ready")
        s_p2 = sem("pair_sums_done")
        s_p2out = sem("pair_sums_stored")
        s_ztop = sem("z_top_copies")
        s_z2 = sem("z2_done")
        s_z2out = sem("z2_stored")
        s_dense = sem("dense_loaded")
        s_h1 = sem("h1_done")
        s_h1out = sem("h1_stored")
        s_h2 = sem("h2_done")
        s_h2out = sem("h2_stored")
        s_y = sem("y_done")
        s_yout = sem("y_copied")
        s_stored = sem("y_written")

        s_met = sem("transposes_begun")
        s_begun = sem("gathers_begun")

        def some(count):
            return not isinstance(count, int) or count > 0

        def tile(q, n):
            return slice((2 * n + q) * P, (2 * n + q + 1) * P)

        block = ctx.enter_context(nc.Block())

        @block.sync
        def _(sp):
            sp.dma_start(ids[:], t["ids"][0:GROUP, :]).then_inc(s_ids, 16)
            sp.dma_start(ident[:], t["ident"]).then_inc(s_const, 16)
            sp.dma_start(own_row[:], t["own_row"]).then_inc(s_const, 16)
            sp.dma_start(bias0[:], t["b0"]).then_inc(s_const, 16)
            sp.dma_start(bias1[:], t["b1"].to_broadcast([P, H])).then_inc(s_const, 16)
            sp.dma_start(bias2[:], t["b2"]).then_inc(s_const, 16)
            sp.dma_start(w1_raw[:, 0:NF, :], t["w1"]).then_inc(s_w1, 16)
            sp.dma_start(w0[:], t["w0"]).then_inc(s_w0, 16)
            sp.dma_start(w0_mirror[:], t["w0_mirror"]).then_inc(s_w0, 16)
            sp.dma_start(w2[:], t["w2"]).then_inc(s_top_w, 16)
            sp.dma_start(wt1[:], t["wt1"]).then_inc(s_top_w, 16)
            sp.dma_start(wt1_dense[:], t["wt1_dense"]).then_inc(s_top_w, 16)
            sp.dma_start(wt2[:], t["wt2"]).then_inc(s_top_w, 16)
            sp.dma_start(wt3[:], t["wt3"]).then_inc(s_top_w, 16)
            sp.dma_start(bt1[:], t["bt1"]).then_inc(s_top_w, 16)
            sp.dma_start(bt2[:], t["bt2"]).then_inc(s_top_w, 16)

            def shift(m):
                sp.wait_ge(s_x0, m + 1)
                for c in range(CHUNKS0):
                    for i, s in enumerate(shifts0(c)):
                        sp.dma_start(x0_shifted[i * NF:(i + 1) * NF, c, :],
                                     x0[s:s + NF, :]).then_inc(s_shifted[c], 16)

            def group(g, first, last):
                n = BLOCKS * g
                if not last:
                    sp.wait_ge(s_gathered, (g + 1) * NF * 16)
                    sp.dma_start(ids[:], t["ids"][bass.ds((g + 1) * GROUP, GROUP), :]).then_inc(s_ids, 16)
                for blk in range(BLOCKS - 1):
                    shift(n + blk + 1)
                if not first:
                    sp.wait_ge(s_h1, g)
                sp.dma_start(dense[:], t["dense"][:, bass.ds(g * GROUP, GROUP)]).then_inc(s_dense, 16)
                if not last:
                    shift(n + BLOCKS)
                if not first:
                    sp.wait_ge(s_yout, g)
                    sp.dma_start(t["y"][:, bass.ds((g - 1) * GROUP, GROUP)], y[:]).then_inc(s_stored, 16)

            shift(0)
            group(0, True, False)
            with sp.Fori(1, GROUPS - 1) as g:
                group(g, False, False)
            group(GROUPS - 1, False, True)
            sp.wait_ge(s_yout, GROUPS)
            sp.dma_start(t["y"][:, B - GROUP:B], y[:]).then_inc(s_stored, 16)
            sp.wait_ge(s_stored, 16 * GROUPS)

        @block.gpsimd
        def _(pool):
            def gather(fields):
                for f in fields:
                    pool.indirect_dma_start(
                        out=gathered[:, f, :], out_offset=None, in_=t[f"tbl_{f}"],
                        in_offset=bass.IndirectOffsetOnAxis(ap=ids[:, f:f + 1].bitcast(U32), axis=0),
                    ).then_inc(s_gathered, 16)

            def spread(par, m):
                pool.wait_ge(s_x0t, m + 1)
                if some(TILES * (m - 1)):
                    pool.wait_ge(s_p2, TILES * (m - 1))
                for i in range(TILES):
                    ins = pool.tensor_tensor(
                        x0_blocks[par][:, i, 0:NF, :],
                        x0_t[par][:, i, :].unsqueeze(2).to_broadcast([P, NF, TILE]),
                        own_row[:].unsqueeze(1).to_broadcast([P, NF, TILE]), ALU.mult)
                ins.then_inc(s_blocks, 1)

            def sums_early(u, i):
                k = 10 * u
                for q, x in enumerate(terms[i]):
                    pool.wait_ge(s_folds, 4 * u + 1 + q)
                    pool.wait_ge(s_term, 2 * TERMS * u + ACT_UPTO[6] - 4 * (1 - q))
                    pool.tensor_tensor(x[:, 0:4, :], x[:, 0:4, :], x[:, 8:12, :], ALU.add).then_inc(s_tree, 1)
                for q, x in enumerate(terms[i]):
                    pool.wait_ge(s_tree, k + 1 + q)
                    pool.tensor_tensor(x[:, 0:2, :], x[:, 0:2, :], x[:, 2:4, :], ALU.add).then_inc(s_tree, 1)
                for q, x in enumerate(terms[i]):
                    pool.wait_ge(s_tree, k + 3 + q)
                    pool.tensor_tensor(x[:, 0, :], x[:, 0, :], x[:, 1, :], ALU.add).then_inc(s_tree, 1)

            def sums_late(u, i):
                k = 10 * u
                for q, x in enumerate(terms[i]):
                    pool.wait_ge(s_folds, 4 * u + 3 + q)
                    pool.tensor_tensor(x[:, 12:14, :], x[:, 12:14, :], x[:, 14:16, :], ALU.add).then_inc(s_tree, 1)
                for q, x in enumerate(terms[i]):
                    pool.wait_ge(s_tree, k + 7 + q)
                    pool.tensor_tensor(x[:, 12, :], x[:, 12, :], x[:, 13, :], ALU.add).then_inc(s_tree, 1)
                for q, x in enumerate(terms[i]):
                    pool.wait_ge(s_tree, k + 9 + q)
                    pool.tensor_tensor(x[:, 0, :], x[:, 0, :], x[:, 12, :], ALU.add).then_inc(s_x2, 1)

            pool.wait_ge(s_ids, 16)
            gather(range(NF))
            pool.wait_ge(s_const, 16 * 5)
            for par in range(2):
                for i in range(TILES):
                    pool.tensor_copy(x0_blocks[par][:, i, NF, :], own_row[:]).then_inc(s_ones, 1)
            spread(0, 0)

            def group(g, last):
                for blk in range(BLOCKS):
                    n = BLOCKS * g + blk
                    for p in range(PAIRS):
                        i = PAIRS * blk + p
                        if not last and i * GATHERS < NF:
                            if i == 0:
                                pool.wait_ge(s_ids, 16 * (g + 2))
                                pool.wait_ge(s_erows, g + 1)
                                pool.sem_inc(s_begun, 1)
                            gather(range(i * GATHERS, min(NF, (i + 1) * GATHERS)))
                        sums_early(PAIRS * n + p, p)
                        sums_late(PAIRS * n + p, p)
                        if p == 0 and not (last and blk == BLOCKS - 1):
                            spread((blk + 1) % 2, n + 1)

            group(0, False)
            with pool.Fori(1, GROUPS - 1) as g:
                group(g, False)
            group(GROUPS - 1, True)

        @block.scalar
        def _(act):
            def erows(g):
                act.wait_ge(s_gathered, (g + 1) * NF * 16)
                if some(BLOCKS * g):
                    act.wait_ge(s_turned, BLOCKS * g)
                act.activation(e_rows[:].rearrange("p d (r j) -> p d r j", r=3),
                               gathered[:].rearrange("p j d -> p d j").unsqueeze(2).to_broadcast([P, D, 3, NF]),
                               ACT.Copy).then_inc(s_erows, 1)

            def store_x0(m):
                act.wait_ge(s_turned, m + 1)
                if some(CHUNKS0 * m):
                    act.wait_ge(s_prods, CHUNKS0 * m)
                src = ps_misc[0:ROWS0, :].rearrange("p (d b) -> p b d", d=D)
                act.activation(x0[:].rearrange("p (b d) -> p b d", d=D), src, ACT.Copy).then_inc(s_x0, 1)

            def store_x0t(par, m):
                act.wait_ge(s_turned_t, m + 1)
                act.activation(x0_t[par][:].rearrange("p i j -> p (i j)"), ps_misc[:, 0:TILES * NF],
                               ACT.Copy).then_inc(s_x0t, 1)

            def store_x1(par, m):
                act.wait_ge(s_l0, CHUNKS0 * (m + 1))
                if some(m):
                    act.wait_ge(s_z0, m)
                act.activation(x1_hi[par][:], ps_x1[:], ACT.Identity, bias=bias0[:]).then_inc(s_x1hi, 1)
                act.activation(x1[:], ps_x1[:], ACT.Identity, bias=bias0[:]).then_inc(s_x1, 1)

            def store_pair_sums(i, col):
                act.wait_ge(s_p2, i + 1)
                act.activation(pair_sums[:, :, bass.ds(col, TILE)],
                               ps_misc[:, 0:NP2 * TILE].rearrange("p (j b) -> p j b", b=TILE),
                               ACT.Copy).then_inc(s_p2out, 1)

            def multiply(v, c, p, par):
                for q in range(2):
                    act.wait_ge(s_part, 2 * v + 1 + q)
                    for n, j in enumerate(FIELDS[c]):
                        act.activation(terms[p][q][:, ACT_UPTO[c] // 2 + n, :], parts[bank(c, q)][:, n * H:(n + 1) * H],
                                       ACT.Copy, scale=x0_t[par][:, 2 * p + q, j:j + 1]).then_inc(s_term, 1)

            def store_z1(g):
                act.wait_ge(s_p2out, (g + 1) * GROUP // TILE)
                act.activation(z_top[:, 1, :], pair_sums[:, NF, :], ACT.Copy).then_inc(s_ztop, 1)

            def store_z2(g):
                act.wait_ge(s_z2, g + 1)
                act.activation(z_top[:, 2, :], ps_top[:, 0:GROUP], ACT.Identity,
                               bias=bias2_sum[:]).then_inc(s_z2out, 1)

            def store_h1(g):
                act.wait_ge(s_h1, g + 1)
                for i in range(4):
                    act.activation(h1[:, i, :], ps_top[:, i * GROUP:(i + 1) * GROUP], ACT.Relu,
                                   bias=bt1[:, i:i + 1]).then_inc(s_h1out, 1)

            def store_h2(g):
                act.wait_ge(s_h2, g + 1)
                for i in range(2):
                    act.activation(h2[:, i, :], ps_top[:, i * GROUP:(i + 1) * GROUP], ACT.Relu,
                                   bias=bt2[:, i:i + 1]).then_inc(s_h2out, 1)

            def store_y(g):
                act.wait_ge(s_y, g + 1)
                if some(16 * g):
                    act.wait_ge(s_stored, 16 * g)
                act.activation(y[:], ps_top[0:1, 0:GROUP], ACT.Copy).then_inc(s_yout, 1)

            act.wait_ge(s_const, 16 * 5)
            act.mul(bias2_sum[:], bias2[:], float(D)).then_inc(s_b2, 1)
            act.wait_ge(s_b2, 1)
            act.wait_ge(s_w1, 16)
            act.activation(w1_hi[:], w1_raw[:, 0:NF, :], ACT.Copy).then_inc(s_w1hi, 1)
            erows(0)
            store_x0(0)
            store_x0t(0, 0)
            store_x1(0, 0)

            def group(g, first, last):
                for blk in range(BLOCKS):
                    n = BLOCKS * g + blk
                    more = not (last and blk == BLOCKS - 1)
                    for s in range(STEPS):
                        p, c = divmod(s, CHUNKS)
                        if c in ACT_CHUNKS:
                            multiply(STEPS * n + s, c, p, blk % 2)
                        if s == 0 and more:
                            store_x0(n + 1)
                        if s in (7, 8) and not (first and blk == 0):
                            col = (BLOCK * blk - BLOCK + (s - 5) * TILE) % GROUP
                            store_pair_sums(TILES * n - 9 + s, col)
                        if s == 4 and more:
                            store_x0t((blk + 1) % 2, n + 1)
                        if s == 8 and blk == 0 and not first:
                            store_z1(g - 1)
                        if s == 16 and more:
                            store_x1((blk + 1) % 2, n + 1)
                        if s in (17, 18):
                            store_pair_sums(TILES * n + s - 17, BLOCK * blk + (s - 17) * TILE)
                        if s == 14 and blk == 2 and not last:
                            erows(g + 1)
                        if s == 6 and blk == 3:
                            act.wait_ge(s_z0, n + 1)
                            if not first:
                                act.wait_ge(s_h1, g)
                            act.activation(z_top[:, 0, :], z0[:], ACT.Copy).then_inc(s_ztop, 1)
                        if not first:
                            if blk == 0 and s == 18:
                                store_z2(g - 1)
                            if blk == 1 and s == TOP1_AT[-1] + 1:
                                store_h1(g - 1)
                            if blk == 2 and s == 11:
                                store_h2(g - 1)
                            if blk == 3 and s == 8:
                                store_y(g - 1)

            group(0, True, False)
            with act.Fori(1, GROUPS - 1) as g:
                group(g, False, False)
            group(GROUPS - 1, False, True)
            for q in range(2):
                store_pair_sums(B // TILE - 2 + q, GROUP - (2 - q) * TILE)
            store_z1(GROUPS - 1)
            store_z2(GROUPS - 1)
            store_h1(GROUPS - 1)
            store_h2(GROUPS - 1)
            store_y(GROUPS - 1)

        @block.vector
        def _(dve):
            def product(m, c):
                k = CHUNKS0 * m + c
                dve.wait_ge(s_shifted[c], 16 * len(shifts0(c)) * (m + 1))
                if c == 0:
                    dve.wait_ge(s_x0, m + 1)
                if c >= PROD_BUFS:
                    dve.wait_ge(s_l0, k + 1 - PROD_BUFS)
                elif some(m):
                    dve.wait_ge(s_l0, CHUNKS0 * m)
                r = rows0(c)
                dve.tensor_tensor(prods[c % PROD_BUFS][0:r, :], x0_shifted[0:r, c, :], x0[0:r, :], ALU.mult).then_inc(s_prods, 1)

            def split_x1(par, m):
                dve.wait_ge(s_x1, m + 1)
                dve.wait_ge(s_x1hi, m + 1)
                dve.tensor_tensor(x1_lo[par][:], x1[:], x1_hi[par][:].bitcast(F32),
                                  ALU.subtract).then_inc(s_x1lo, 1)

            def sum_x1(m, col):
                dve.tensor_reduce(z0[:, bass.ds(col, BLOCK)], x1[:].rearrange("p (b d) -> p b d", d=D),
                                  AX.X, ALU.add).then_inc(s_z0, 1)

            def fold_early(u, p):
                for q, x in enumerate(terms[p]):
                    dve.wait_ge(s_term, 2 * TERMS * u + ACT_UPTO[4] - 4 * (1 - q))
                    dve.tensor_tensor(x[:, 0:4, :], x[:, 0:4, :], x[:, 4:8, :], ALU.add).then_inc(s_folds, 1)

            def fold_late(u, p):
                for q, x in enumerate(terms[p]):
                    dve.wait_ge(s_term, 2 * TERMS * (u + 1) - 3 * (1 - q))
                    dve.wait_ge(s_acc, PER_PAIR * (u + 1) - 1 + q)
                    dve.tensor_tensor(x[:, 12:16, :], x[:, 12:16, :], x[:, 16:20, :], ALU.add).then_inc(s_folds, 1)

            def add_terms(u, c, p, par):
                k = PER_PAIR * u + DVE_UPTO[c]
                for n, j in enumerate(FIELDS[c]):
                    for q in range(2):
                        if n == 0:
                            dve.wait_ge(s_part, 2 * (CHUNKS * u + c) + 1 + q)
                        if c or n:
                            dve.wait_ge(s_acc, k + 2 * n + q - 1)
                        total = terms[p][q][:, TERMS, :]
                        dve.scalar_tensor_tensor(
                            out=total, in0=parts[bank(c, q)][:, n * H:(n + 1) * H],
                            scalar=x0_t[par][:, 2 * p + q, j:j + 1], in1=total if c or n else bias1[:],
                            op0=ALU.mult, op1=ALU.add).then_inc(s_acc, 1)

            dve.wait_ge(s_w0, 32)
            dve.tensor_tensor(w0[:], w0[:], w0_mirror[:], ALU.add).then_inc(s_w0sum, 1)
            dve.wait_ge(s_w1hi, 1)
            dve.tensor_tensor(w1_lo[:], w1_raw[:, 0:NF, :], w1_hi[:].bitcast(F32), ALU.subtract).then_inc(s_w1lo, 1)
            for c in range(CHUNKS0):
                product(0, c)
            split_x1(0, 0)
            sum_x1(0, 0)
            dve.wait_ge(s_const, 16 * 5)
            dve.wait_ge(s_x0t, 1)

            def group(g, first, last):
                for blk in range(BLOCKS):
                    n = BLOCKS * g + blk
                    more = not (last and blk == BLOCKS - 1)
                    for s in range(STEPS):
                        p, c = divmod(s, CHUNKS)
                        if c not in ACT_CHUNKS:
                            add_terms(PAIRS * n + p, c, p, blk % 2)
                        if c == 0 and not (first and blk == 0 and s == 0):
                            fold_late(PAIRS * n + p - 1, 1 - p)
                        if c == 4:
                            fold_early(PAIRS * n + p, p)
                        if not more:
                            continue
                        for c0 in PRODUCTS_AT.get(s, ()):
                            product(n + 1, c0)
                        if s == 17:
                            split_x1((blk + 1) % 2, n + 1)
                        if s == 18:
                            if blk == BLOCKS - 1:
                                dve.wait_ge(s_ztop, 2 * g + 1)
                            sum_x1(n + 1, BLOCK * ((blk + 1) % BLOCKS))

            group(0, True, False)
            with dve.Fori(1, GROUPS - 1) as g:
                group(g, False, False)
            group(GROUPS - 1, False, True)
            fold_late(PAIRS * BLOCKS * GROUPS - 1, 1)

        @block.tensor
        def _(pe):
            def turn_x0(blk, m):
                pe.wait_ge(s_erows, m // BLOCKS + 1 if isinstance(m, int) else erow_count[0])
                if some(m):
                    pe.wait_ge(s_x0t, m)
                if some(TILES * (m - 1) - 2):
                    pe.wait_ge(s_p2out, TILES * (m - 1) - 2)
                pe.sem_inc(s_met, 1)
                r = slice(BLOCK * blk, BLOCK * (blk + 1))
                for d in range(D):
                    ins = pe.transpose(ps_misc[0:ROWS0, d * BLOCK:(d + 1) * BLOCK], e_rows[r, d, :], ident[r, r])
                ins.then_inc(s_turned, 1)

            def turn_x0t(m):
                pe.wait_ge(s_x0, m + 1)
                pe.sem_inc(s_met, 1)
                for i in range(TILES):
                    ins = pe.transpose(ps_misc[:, i * NF:(i + 1) * NF], x0[0:NF, i * P:(i + 1) * P],
                                       ident[0:NF, 0:NF])
                ins.then_inc(s_turned_t, 1)

            def layer0(m, c):
                pe.wait_ge(s_prods, CHUNKS0 * m + c + 1)
                if c == 0:
                    if some(m):
                        pe.wait_ge(s_x1, m)
                r = rows0(c)
                pe.matmul(ps_x1[:], w0[0:r, c, :], prods[c % PROD_BUFS][0:r, :], start=(c == 0),
                          stop=(c == CHUNKS0 - 1)).then_inc(s_l0, 1)

            def layer1(u, c, p, par):
                w = len(FIELDS[c]) * H
                f = slice(FIELDS[c][0], FIELDS[c][-1] + 1)
                for q in range(2):
                    q2 = 1 - q
                    back = (PARTS + 1 - 2 * q) // 2
                    c2, u2 = (c - back) % CHUNKS, u - (c < back)
                    if c2 in ACT_CHUNKS:
                        count = 2 * TERMS * u2 + ACT_UPTO[c2 + 1] - len(FIELDS[c2]) * (1 - q2)
                        if some(count):
                            pe.wait_ge(s_term, count)
                    else:
                        count = PER_PAIR * u2 + DVE_UPTO[c2 + 1] - 1 + q2
                        if some(count):
                            pe.wait_ge(s_acc, count)
                    out = parts[bank(c, q)][:, 0:w]
                    hi = x1_hi[par][:, tile(q, p)]
                    lo = x1_lo[par][:, tile(q, p)]
                    pe.matmul(out, hi, w1_hi[:, f, :], start=True, stop=False)
                    pe.matmul(out, hi, w1_lo[:, f, :], start=False, stop=False)
                    if c == 0 and p == 0 and q == 0:
                        pe.wait_ge(s_x1lo, u // PAIRS + 1 if isinstance(u, int) else block_count[0])
                    pe.matmul(out, lo, w1_hi[:, f, :], start=False, stop=True).then_inc(s_part, 1)

            def sum_pairs(i, par, k, p, q, m):
                pe.wait_ge(s_x2, i + 1)
                if some(i):
                    pe.wait_ge(s_p2out, i)
                pe.matmul(ps_misc[:, 0:NP2 * TILE], terms[p][q][:, 0, :],
                          x0_blocks[par][:, k, :, :].rearrange("p j b -> p (j b)"), start=True,
                          stop=True).then_inc(s_p2, 1)

            def z2(g, js):
                if js[0] == 0:
                    pe.wait_ge(s_p2out, (g + 1) * GROUP // TILE)
                    if some(g):
                        pe.wait_ge(s_yout, g)
                for j in js:
                    ins = pe.matmul(ps_top[:, 0:GROUP], w2[:, j, :], pair_sums[:, j, :], start=(j == 0),
                                    stop=(j == NF - 1))
                if js[-1] == NF - 1:
                    ins.then_inc(s_z2, 1)

            def top1(g, i, last):
                if i == 0:
                    pe.wait_ge(s_z2out, g + 1)
                    pe.wait_ge(s_ztop, 2 * g + 2)
                    pe.wait_ge(s_dense, 16 * (g + 1))
                out = ps_top[:, i * GROUP:(i + 1) * GROUP]
                for k in range(3):
                    pe.matmul(out, wt1[:, k, i * P:(i + 1) * P], z_top[:, k, :], start=(k == 0), stop=False)
                ins = pe.matmul(out, wt1_dense[:, i * P:(i + 1) * P], dense[:], start=False, stop=True)
                if i == 3:
                    ins.then_inc(s_h1, 1)

            def top2(g, i):
                if i == 0:
                    pe.wait_ge(s_h1out, 4 * (g + 1))
                for k in range(4):
                    ins = pe.matmul(ps_top[:, i * GROUP:(i + 1) * GROUP], wt2[:, k, i * P:(i + 1) * P],
                                    h1[:, k, :], start=(k == 0), stop=(k == 3))
                if i == 1:
                    ins.then_inc(s_h2, 1)

            def top3(g):
                pe.wait_ge(s_h2out, 2 * (g + 1))
                for k in range(2):
                    ins = pe.matmul(ps_top[0:1, 0:GROUP], wt3[:, k:k + 1], h2[:, k, :], start=(k == 0),
                                    stop=(k == 1))
                ins.then_inc(s_y, 1)

            erow_count = [1]
            block_count = [1]
            pe.wait_ge(s_const, 16 * 5)
            turn_x0(0, 0)
            turn_x0t(0)
            pe.wait_ge(s_w0sum, 1)
            for c in range(CHUNKS0):
                layer0(0, c)
            pe.wait_ge(s_x1hi, 1)
            pe.wait_ge(s_w1lo, 1)
            pe.wait_ge(s_top_w, 16 * 7)

            Z2_STEP = 6

            def group(g, first, last):
                for blk in range(BLOCKS):
                    n = BLOCKS * g + blk
                    more = not (last and blk == BLOCKS - 1)
                    par, nxt = blk % 2, (blk + 1) % 2
                    erow_count[0] = g + 1 + (blk + 1) // BLOCKS
                    block_count[0] = n + 1
                    for s in range(STEPS):
                        p, c = divmod(s, CHUNKS)
                        layer1(PAIRS * n + p, c, p, par)
                        if s == 0 and more:
                            turn_x0((blk + 1) % BLOCKS, n + 1)
                        if more:
                            for c0 in LAYER0_AT.get(s, ()):
                                layer0(n + 1, c0)
                        if s in (7, 8) and not (first and blk == 0):
                            if s == 7 and more:
                                pe.wait_ge(s_x0t, n + 2)
                            sum_pairs(TILES * n - 9 + s, nxt, s - 5, 1, s - 7, n - 1)
                        if s == 3 and more:
                            turn_x0t(n + 1)
                        if s in (17, 18):
                            if s == 17:
                                pe.wait_ge(s_blocks, n + 1)
                            sum_pairs(TILES * n + s - 17, par, s - 17, 0, s - 17, n)
                        if not first:
                            if blk == 0 and 10 <= s < 17:
                                z2(g - 1, range((s - 10) * Z2_STEP, min(NF, (s - 9) * Z2_STEP)))
                            if blk == 1 and s in TOP1_AT:
                                top1(g - 1, TOP1_AT.index(s), last)
                            if blk == 2 and s in (5, 7):
                                top2(g - 1, (s - 5) // 2)
                            if blk == 3 and s == 5:
                                top3(g - 1)
                    if more:
                        pe.wait_ge(s_x1hi, n + 2)

            group(0, True, False)
            with pe.Fori(1, GROUPS - 1) as g:
                group(g, False, False)
            group(GROUPS - 1, False, True)
            g = GROUPS - 1
            for q in range(2):
                sum_pairs(B // TILE - 2 + q, 1, 2 + q, 1, q, 0)
            z2(g, range(NF))
            for i in range(4):
                top1(g, i, True)
            for i in range(2):
                top2(g, i)
            top3(g)


def kernel(**inputs):
    import concourse.bacc as bacc
    from concourse.bass_utils import run_bass_kernel_spmd as run

    x = {k: np.asarray(v) for k, v in inputs.items()}
    first = np.tile(np.arange(NF), 3 * CHUNKS0)
    shift = np.repeat(np.arange(3 * CHUNKS0), NF)
    second = (first + shift) % NF
    W0 = x["L0_rec_W0"].reshape(H, NF, NF)
    used = (shift < SHIFTS)[:, None]
    w0 = np.where(used, W0[:, first, second].T, np.float32(0))
    mirror = np.where(used & (shift > 0)[:, None], W0[:, second, first].T, np.float32(0))

    def chunks0(a):
        return a.reshape(CHUNKS0, ROWS0, H).transpose(1, 0, 2)

    arrays = {
        "ids": x["ids"],
        "dense": x["dense_ctx"].T,
        "ident": np.eye(P, dtype=np.float32),
        "own_row": np.repeat(np.eye(TILE, dtype=np.float32), D, axis=0),
        "w0": chunks0(w0),
        "w0_mirror": chunks0(mirror),
        "w1": x["L0_rec_W1"].reshape(H, NF, H).transpose(2, 1, 0),
        "w2": x["L0_rec_W2"].reshape(H, NF, H).transpose(2, 1, 0),
        "b0": x["L0_rec_b0"].reshape(H, 1),
        "b1": x["L0_rec_b1"].reshape(1, H),
        "b2": x["L0_rec_b2"].reshape(H, 1),
        "wt1": x["W_top1"][:3 * P].reshape(3, P, 512).transpose(1, 0, 2),
        "wt1_dense": x["W_top1"][3 * P:],
        "wt2": x["W_top2"].reshape(4, P, 256).transpose(1, 0, 2),
        "wt3": x["W_top3"].reshape(2, P).T,
        "bt1": x["b_top1"].reshape(4, P).T,
        "bt2": x["b_top2"].reshape(2, P).T,
    }
    arrays.update({f"tbl_{f}": x[f"tbl_{f}"] for f in range(NF)})
    nc = bacc.Bacc("TRN2", target_bir_lowering=False, num_devices=1)
    given, t = {}, {}
    for name, a in arrays.items():
        a = np.ascontiguousarray(a)
        given[f"in_{name}"] = a
        t[name] = nc.dram_tensor(f"in_{name}", a.shape, mybir.dt.from_np(a.dtype), kind="ExternalInput").ap()
    t["y"] = nc.dram_tensor("out_y", (1, B), F32, kind="ExternalOutput").ap()
    build(nc, t)
    r = run(nc, [given], core_ids=[0])
    return r.results[0]["out_y"].reshape(B, 1)
```

```python
from contextlib import ExitStack

import numpy as np
import concourse.bass as bass
from concourse import mybir

F32 = mybir.dt.float32
F32R = mybir.dt.float32r
I32 = mybir.dt.int32
U32 = mybir.dt.uint32
ALU = mybir.AluOpType
ACT = mybir.ActivationFunctionType
AX = mybir.AxisListType

P = 128
NF = 39
D = 16
H = 128
B = 1024
GROUP = 128
GROUPS = B // GROUP
BLOCK = 32
BLOCKS = GROUP // BLOCK
COLS = BLOCK * D
TILE = P // D
TILES = BLOCK // TILE
PAIRS = TILES // 2
CHUNKS = 10
STEPS = PAIRS * CHUNKS
SHIFTS = NF // 2 + 1
ROWS0 = 3 * NF
CHUNKS0 = -(-SHIFTS // 3)
NP2 = NF + 1

FIELDS = [range(4 * c, min(4 * c + 4, NF)) for c in range(CHUNKS)]
ACT_CHUNKS = (1, 3, 5, 7, 9)
TERMS = sum(len(FIELDS[c]) for c in ACT_CHUNKS)
DVE_UPTO, ACT_UPTO = [0], [0]
for c, f in enumerate(FIELDS):
    DVE_UPTO.append(DVE_UPTO[-1] + 2 * len(f) * (c not in ACT_CHUNKS))
    ACT_UPTO.append(ACT_UPTO[-1] + 2 * len(f) * (c in ACT_CHUNKS))
PER_PAIR = DVE_UPTO[-1]
PRODUCT_AT = {2: 1, 4: 2, 6: 3, 8: 4, 12: 5, 13: 6}
HIGH_AT = {0: 0, 3: 1, 5: 2, 7: 3, 9: 4, 13: 5, 14: 6}
LOW_AT = {2: 0, 4: 1, 6: 2, 8: 3, 10: 4, 14: 5, 15: 6}
LAYER0_AT = {5: [0], 7: [1], 9: [2], 11: [3], 13: [4], 16: [5, 6]}
TOP1_AT = [2, 4, 6, 13]
PARTS = 5
EARLY = [range(0, 5), range(5, 10)]
REST = [range(i, min(i + 6, NF)) for i in range(10, NF, 6)]


def shifts0(c):
    return range(3 * c, min(3 * c + 3, SHIFTS))


def bank(c, q):
    return (2 * c + q) % PARTS


def rows0(c):
    return NF * len(shifts0(c))


def build(nc, t):
    ctx = ExitStack()
    with ctx:
        def sb(name, shape, dt=F32):
            return ctx.enter_context(nc.sbuf_tensor(name, shape, dt))

        def ps(name, shape):
            return ctx.enter_context(nc.psum_tensor(name, shape, F32))

        def sem(name):
            return ctx.enter_context(nc.semaphore(name))

        w1_hi = sb("w1_hi", [P, NF, H], F32R)
        w1_lo = sb("w1_lo", [P, NF, H], F32R)
        w2 = sb("w2", [P, NF, H])
        w0_hi = sb("w0_hi", [ROWS0, CHUNKS0, H], F32R)
        w0_lo = sb("w0_lo", [ROWS0, CHUNKS0, H], F32R)
        ident = sb("ident", [P, P])
        own_row = sb("own_row", [P, TILE])
        bias0 = sb("bias0", [P, 1])
        bias1 = sb("bias1", [P, H])
        bias2 = sb("bias2", [P, 1])
        bias2_sum = sb("bias2_sum", [P, 1])
        wt1 = sb("wt1", [P, 3, 512])
        wt1_dense = sb("wt1_dense", [D, 512])
        wt2 = sb("wt2", [P, 4, 256])
        wt3 = sb("wt3", [P, 2])
        bt1 = sb("bt1", [P, 4])
        bt2 = sb("bt2", [P, 2])
        ids = sb("ids", [P, NF], I32)
        gathered = sb("gathered", [P, NF, D])
        e_rows = sb("e_rows", [P, D, ROWS0])
        x0 = sb("x0", [ROWS0, COLS])
        x0_shifted = sb("x0_shifted", [ROWS0, CHUNKS0, COLS])
        x0_t = [sb(f"x0_t{i}", [P, TILES, NF]) for i in range(2)]
        x0_blocks = [sb(f"x0_blocks{i}", [P, TILES, NP2, TILE]) for i in range(2)]
        prods = [sb(f"prods{i}", [ROWS0, COLS]) for i in range(2)]
        prods_hi = [sb(f"prods_hi{i}", [ROWS0, COLS], F32R) for i in range(2)]
        prods_lo = [sb(f"prods_lo{i}", [ROWS0, COLS], F32R) for i in range(2)]
        x1 = sb("x1", [P, COLS])
        x1_hi = [sb(f"x1_hi{i}", [P, COLS], F32R) for i in range(2)]
        x1_lo = [sb(f"x1_lo{i}", [P, COLS], F32R) for i in range(2)]
        terms = [[sb(f"terms{i}{q}", [P, TERMS + 1, H]) for q in range(2)] for i in range(2)]
        w0_raw, w0_mirror = (x[0:ROWS0, 0:CHUNKS0, :] for x in terms[0])
        perms_raw = terms[1][0][0:NF, 0:CHUNKS0, 0:ROWS0]
        perms = [x1_hi[0], x1_lo[0]]
        PERMS = COLS // ROWS0
        x0_hi, x0_lo = x1_hi[1], x1_lo[1]
        pair_sums = sb("pair_sums", [P, NP2, GROUP])
        w1_raw = pair_sums
        z0 = sb("z0", [P, GROUP])
        z_top = sb("z_top", [P, 3, GROUP])
        dense = sb("dense", [D, GROUP])
        h1 = sb("h1", [P, 4, GROUP])
        h2 = sb("h2", [P, 2, GROUP])
        y = sb("y", [1, GROUP])

        parts = [ps(f"part{i}", [P, 512]) for i in range(PARTS)]
        ps_x1 = ps("ps_x1", [P, 512])
        ps_misc = ps("ps_misc", [P, 512])
        ps_top = ps("ps_top", [P, 512])

        s_w1 = sem("w1_loaded")
        s_w0 = sem("w0_loaded")
        s_const = sem("constants_loaded")
        s_top_w = sem("top_weights_loaded")
        s_ids = sem("ids_loaded")
        s_gathered = sem("tables_gathered")
        s_w1hi = sem("w1_hi_ready")
        s_w1lo = sem("w1_lo_ready")
        s_w0sum = sem("w0_folded")
        s_w0hi = sem("w0_hi_ready")
        s_w0lo = sem("w0_lo_ready")
        s_b2 = sem("bias2_sum_ready")
        s_ones = sem("own_row_columns_ready")
        s_erows = sem("e_rows_ready")
        s_turned = sem("x0_turned")
        s_x0 = sem("x0_ready")
        s_turned_t = sem("x0_t_turned")
        s_x0t = sem("x0_t_ready")
        s_blocks = sem("x0_blocks_ready")
        s_shifted = [sem(f"x0_shifted{c}_loaded") for c in range(CHUNKS0)]
        s_prods = sem("products_ready")
        s_high = sem("products_hi_ready")
        s_low = sem("products_lo_ready")
        s_l0 = sem("layer0_matmuls")
        s_x1 = sem("x1_ready")
        s_x1hi = sem("x1_hi_ready")
        s_x1lo = sem("x1_lo_ready")
        s_z0 = sem("z0_ready")
        s_part = sem("part_full")
        s_acc = sem("vector_terms_added")
        s_term = sem("scalar_terms_ready")
        s_tree = sem("gpsimd_sums")
        s_folds = sem("vector_folds")
        s_x2 = sem("x2_ready")
        s_p2 = sem("pair_sums_done")
        s_p2out = sem("pair_sums_stored")
        s_ztop = sem("z_top_copies")
        s_z2 = sem("z2_done")
        s_z2out = sem("z2_stored")
        s_dense = sem("dense_loaded")
        s_h1 = sem("h1_done")
        s_h1out = sem("h1_stored")
        s_h2 = sem("h2_done")
        s_h2out = sem("h2_stored")
        s_y = sem("y_done")
        s_yout = sem("y_copied")
        s_stored = sem("y_written")

        s_perms = sem("perms_loaded")
        s_permsr = sem("perms_rounded")
        s_x0hi = sem("x0_hi_ready")
        s_x0lo = sem("x0_lo_ready")
        s_permuted = sem("x0_permuted")
        s_met = sem("transposes_begun")
        s_begun = sem("gathers_begun")

        def some(count):
            return not isinstance(count, int) or count > 0

        def tile(q, n):
            return slice((2 * n + q) * P, (2 * n + q + 1) * P)

        block = ctx.enter_context(nc.Block())

        @block.sync
        def _(sp):
            sp.dma_start(ids[:], t["ids"][0:GROUP, :]).then_inc(s_ids, 16)
            sp.dma_start(ident[:], t["ident"]).then_inc(s_const, 16)
            sp.dma_start(own_row[:], t["own_row"]).then_inc(s_const, 16)
            sp.dma_start(bias0[:], t["b0"]).then_inc(s_const, 16)
            sp.dma_start(bias1[:], t["b1"].to_broadcast([P, H])).then_inc(s_const, 16)
            sp.dma_start(bias2[:], t["b2"]).then_inc(s_const, 16)
            sp.dma_start(w1_raw[:, 0:NF, :], t["w1"]).then_inc(s_w1, 16)
            sp.dma_start(w0_raw, t["w0"]).then_inc(s_w0, 16)
            sp.dma_start(w0_mirror, t["w0_mirror"]).then_inc(s_w0, 16)
            sp.dma_start(perms_raw, t["perms"]).then_inc(s_perms, 16)
            sp.dma_start(w2[:], t["w2"]).then_inc(s_top_w, 16)
            sp.dma_start(wt1[:], t["wt1"]).then_inc(s_top_w, 16)
            sp.dma_start(wt1_dense[:], t["wt1_dense"]).then_inc(s_top_w, 16)
            sp.dma_start(wt2[:], t["wt2"]).then_inc(s_top_w, 16)
            sp.dma_start(wt3[:], t["wt3"]).then_inc(s_top_w, 16)
            sp.dma_start(bt1[:], t["bt1"]).then_inc(s_top_w, 16)
            sp.dma_start(bt2[:], t["bt2"]).then_inc(s_top_w, 16)

            def shift(m):
                sp.wait_ge(s_x0, m + 1)
                for c in range(CHUNKS0):
                    for i, s in enumerate(shifts0(c)):
                        sp.dma_start(x0_shifted[i * NF:(i + 1) * NF, c, :],
                                     x0[s:s + NF, :]).then_inc(s_shifted[c], 16)

            def group(g, first, last, before_last):
                n = BLOCKS * g
                shift(n + 2)
                shift(n + 3)
                if not (last or before_last):
                    sp.wait_ge(s_gathered, (g + 2) * NF * 16)
                    sp.dma_start(ids[:], t["ids"][bass.ds((g + 2) * GROUP, GROUP), :]).then_inc(s_ids, 16)
                if not last:
                    shift(n + 4)
                if not first:
                    sp.wait_ge(s_h1, g)
                sp.dma_start(dense[:], t["dense"][:, bass.ds(g * GROUP, GROUP)]).then_inc(s_dense, 16)
                if not last:
                    shift(n + 5)
                if not first:
                    sp.wait_ge(s_yout, g)
                    sp.dma_start(t["y"][:, bass.ds((g - 1) * GROUP, GROUP)], y[:]).then_inc(s_stored, 16)

            sp.wait_ge(s_gathered, NF * 16)
            sp.dma_start(ids[:], t["ids"][GROUP:2 * GROUP, :]).then_inc(s_ids, 16)
            shift(1)
            group(0, True, False, False)
            with sp.Fori(1, GROUPS - 2) as g:
                group(g, False, False, False)
            group(GROUPS - 2, False, False, True)
            group(GROUPS - 1, False, True, False)
            sp.wait_ge(s_yout, GROUPS)
            sp.dma_start(t["y"][:, B - GROUP:B], y[:]).then_inc(s_stored, 16)
            sp.wait_ge(s_stored, 16 * GROUPS)

        @block.gpsimd
        def _(pool):
            def gather(fields):
                for f in fields:
                    pool.indirect_dma_start(
                        out=gathered[:, f, :], out_offset=None, in_=t[f"tbl_{f}"],
                        in_offset=bass.IndirectOffsetOnAxis(ap=ids[:, f:f + 1].bitcast(U32), axis=0),
                    ).then_inc(s_gathered, 16)

            def spread(par, m):
                pool.wait_ge(s_x0t, m + 1)
                if some(TILES * (m - 1)):
                    pool.wait_ge(s_p2, TILES * (m - 1))
                for i in range(TILES):
                    ins = pool.tensor_tensor(
                        x0_blocks[par][:, i, 0:NF, :],
                        x0_t[par][:, i, :].unsqueeze(2).to_broadcast([P, NF, TILE]),
                        own_row[:].unsqueeze(1).to_broadcast([P, NF, TILE]), ALU.mult)
                ins.then_inc(s_blocks, 1)

            def sums_early(u, i):
                k = 12 * u
                for q, x in enumerate(terms[i]):
                    pool.wait_ge(s_term, 2 * TERMS * u + ACT_UPTO[4] - 4 * (1 - q))
                    pool.tensor_tensor(x[:, 0:4, :], x[:, 0:4, :], x[:, 4:8, :], ALU.add).then_inc(s_tree, 1)
                for q, x in enumerate(terms[i]):
                    pool.wait_ge(s_tree, k + 1 + q)
                    pool.wait_ge(s_term, 2 * TERMS * u + ACT_UPTO[6] - 4 * (1 - q))
                    pool.tensor_tensor(x[:, 0:4, :], x[:, 0:4, :], x[:, 8:12, :], ALU.add).then_inc(s_tree, 1)
                for q, x in enumerate(terms[i]):
                    pool.wait_ge(s_tree, k + 3 + q)
                    pool.tensor_tensor(x[:, 0:2, :], x[:, 0:2, :], x[:, 2:4, :], ALU.add).then_inc(s_tree, 1)
                for q, x in enumerate(terms[i]):
                    pool.wait_ge(s_tree, k + 5 + q)
                    pool.tensor_tensor(x[:, 0, :], x[:, 0, :], x[:, 1, :], ALU.add).then_inc(s_tree, 1)

            def sums_late(u, i):
                k = 12 * u + 8
                for q, x in enumerate(terms[i]):
                    pool.wait_ge(s_folds, 2 * u + 1 + q)
                    pool.tensor_tensor(x[:, 12:14, :], x[:, 12:14, :], x[:, 14:16, :], ALU.add).then_inc(s_tree, 1)
                for q, x in enumerate(terms[i]):
                    pool.wait_ge(s_tree, k + 1 + q)
                    pool.tensor_tensor(x[:, 12, :], x[:, 12, :], x[:, 13, :], ALU.add).then_inc(s_tree, 1)
                for q, x in enumerate(terms[i]):
                    pool.wait_ge(s_tree, k + 3 + q)
                    pool.tensor_tensor(x[:, 0, :], x[:, 0, :], x[:, 12, :], ALU.add).then_inc(s_x2, 1)

            def ones(par, i):
                pool.tensor_copy(x0_blocks[par][:, i, NF, :], own_row[:]).then_inc(s_ones, 1)

            pool.wait_ge(s_ids, 16)
            gather(range(NF - 10))
            pool.wait_ge(s_const, 16 * 5)
            ones(0, 0)
            gather(range(NF - 10, NF))
            for k in range(1, 2 * TILES):
                ones(k // TILES, k % TILES)
            spread(0, 0)

            def gather_first(g):
                pool.wait_ge(s_ids, 16 * (g + 1))
                pool.wait_ge(s_erows, g)
                pool.sem_inc(s_begun, 1)
                gather(EARLY[0])

            gather_first(1)
            gather(EARLY[1])

            def group(g, last, before_last):
                for blk in range(BLOCKS):
                    n = BLOCKS * g + blk
                    for p in range(PAIRS):
                        i = PAIRS * blk + p
                        if not last and i < len(REST):
                            gather(REST[i])
                        if not last and not before_last and blk == BLOCKS - 1:
                            if p == 0:
                                gather_first(g + 2)
                            else:
                                gather(EARLY[p])
                        sums_early(PAIRS * n + p, p)
                        sums_late(PAIRS * n + p, p)
                        if p == 0 and not (last and blk == BLOCKS - 1):
                            spread((blk + 1) % 2, n + 1)

            group(0, False, False)
            with pool.Fori(1, GROUPS - 2) as g:
                group(g, False, False)
            group(GROUPS - 2, False, True)
            group(GROUPS - 1, True, False)

        @block.scalar
        def _(act):
            def erows(g):
                act.wait_ge(s_gathered, (g + 1) * NF * 16)
                if some(BLOCKS * g):
                    act.wait_ge(s_turned, BLOCKS * g)
                act.activation(e_rows[:].rearrange("p d (r j) -> p d r j", r=3),
                               gathered[:].rearrange("p j d -> p d j").unsqueeze(2).to_broadcast([P, D, 3, NF]),
                               ACT.Copy).then_inc(s_erows, 1)

            def store_x0(m):
                act.wait_ge(s_turned, m + 1)
                if some(CHUNKS0 * m):
                    act.wait_ge(s_prods, CHUNKS0 * m)
                src = ps_misc[0:ROWS0, :].rearrange("p (d b) -> p b d", d=D)
                act.activation(x0[:].rearrange("p (b d) -> p b d", d=D), src, ACT.Copy).then_inc(s_x0, 1)

            def high(m, c):
                k = CHUNKS0 * m + c
                act.wait_ge(s_prods, k + 1)
                if c >= 2:
                    act.wait_ge(s_l0, k - 1)
                elif some(m):
                    act.wait_ge(s_l0, CHUNKS0 * m)
                r = rows0(c)
                act.activation(prods_hi[c % 2][0:r, :], prods[c % 2][0:r, :], ACT.Copy).then_inc(s_high, 1)

            def store_x0t(par, m):
                act.wait_ge(s_turned_t, m + 1)
                act.activation(x0_t[par][:].rearrange("p i j -> p (i j)"), ps_misc[:, 0:TILES * NF],
                               ACT.Copy).then_inc(s_x0t, 1)

            def store_x1(par, m):
                act.wait_ge(s_l0, CHUNKS0 * (m + 1))
                if some(m):
                    act.wait_ge(s_z0, m)
                act.activation(x1_hi[par][:], ps_x1[:], ACT.Identity, bias=bias0[:]).then_inc(s_x1hi, 1)
                act.activation(x1[:], ps_x1[:], ACT.Identity, bias=bias0[:]).then_inc(s_x1, 1)

            def store_pair_sums(i, col):
                act.wait_ge(s_p2, i + 1)
                act.activation(pair_sums[:, :, bass.ds(col, TILE)],
                               ps_misc[:, 0:NP2 * TILE].rearrange("p (j b) -> p j b", b=TILE),
                               ACT.Copy).then_inc(s_p2out, 1)

            def multiply(v, c, p, par):
                for q in range(2):
                    act.wait_ge(s_part, 2 * v + 1 + q)
                    for n, j in enumerate(FIELDS[c]):
                        act.activation(terms[p][q][:, ACT_UPTO[c] // 2 + n, :],
                                       parts[bank(c, q)][:, n * H:(n + 1) * H],
                                       ACT.Copy, scale=x0_t[par][:, 2 * p + q, j:j + 1]).then_inc(s_term, 1)

            def store_z1(g):
                act.wait_ge(s_p2out, (g + 1) * GROUP // TILE)
                act.activation(z_top[:, 1, :], pair_sums[:, NF, :], ACT.Copy).then_inc(s_ztop, 1)

            def store_z2(g):
                act.wait_ge(s_z2, g + 1)
                act.activation(z_top[:, 2, :], ps_top[:, 0:GROUP], ACT.Identity,
                               bias=bias2_sum[:]).then_inc(s_z2out, 1)

            def store_h1(g):
                act.wait_ge(s_h1, g + 1)
                for i in range(4):
                    act.activation(h1[:, i, :], ps_top[:, i * GROUP:(i + 1) * GROUP], ACT.Relu,
                                   bias=bt1[:, i:i + 1]).then_inc(s_h1out, 1)

            def store_h2(g):
                act.wait_ge(s_h2, g + 1)
                for i in range(2):
                    act.activation(h2[:, i, :], ps_top[:, i * GROUP:(i + 1) * GROUP], ACT.Relu,
                                   bias=bt2[:, i:i + 1]).then_inc(s_h2out, 1)

            def store_y(g):
                act.wait_ge(s_y, g + 1)
                if some(16 * g):
                    act.wait_ge(s_stored, 16 * g)
                act.activation(y[:], ps_top[0:1, 0:GROUP], ACT.Copy).then_inc(s_yout, 1)

            act.wait_ge(s_const, 16 * 5)
            act.mul(bias2_sum[:], bias2[:], float(D)).then_inc(s_b2, 1)
            act.wait_ge(s_b2, 1)
            act.wait_ge(s_w1, 16)
            act.activation(w1_hi[:], w1_raw[:, 0:NF, :], ACT.Copy).then_inc(s_w1hi, 1)
            act.wait_ge(s_w0sum, 1)
            act.activation(w0_hi[:], w0_raw, ACT.Copy).then_inc(s_w0hi, 1)
            act.wait_ge(s_perms, 16)
            for i in range(2):
                chunks = range(i * PERMS, min((i + 1) * PERMS, CHUNKS0))
                act.activation(perms[i][0:NF, 0:len(chunks) * ROWS0].rearrange("p (c r) -> p c r", r=ROWS0),
                               perms_raw[:, chunks[0]:chunks[-1] + 1, :], ACT.Copy).then_inc(s_permsr, 1)
            erows(0)
            store_x0(0)
            act.wait_ge(s_x0, 1)
            act.activation(x0_hi[0:NF, :], x0[0:NF, :], ACT.Copy).then_inc(s_x0hi, 1)
            store_x0t(0, 0)
            for c in range(CHUNKS0):
                high(0, c)
            store_x1(0, 0)
            store_x0(1)

            def group(g, first, last):
                for blk in range(BLOCKS):
                    n = BLOCKS * g + blk
                    more = not (last and blk == BLOCKS - 1)
                    for s in range(STEPS):
                        p, c = divmod(s, CHUNKS)
                        if c in ACT_CHUNKS:
                            multiply(STEPS * n + s, c, p, blk % 2)
                        if first and blk == 0 and s == 1:
                            high(1, 0)
                        elif s in HIGH_AT and more and not (first and blk == 0 and s == 0):
                            high(n + 1, HIGH_AT[s])
                        if s == 15 and not (last and blk >= BLOCKS - 2):
                            store_x0(n + 2)
                        if s in (8, 10) and not (first and blk == 0):
                            col = (BLOCK * blk - BLOCK + (s // 2 - 2) * TILE) % GROUP
                            store_pair_sums(TILES * n - 6 + s // 2, col)
                        if s == 4 and more:
                            store_x0t((blk + 1) % 2, n + 1)
                        if s == 10 and blk == 0 and not first:
                            store_z1(g - 1)
                        if s == 16 and more:
                            store_x1((blk + 1) % 2, n + 1)
                        if s in (18, 19):
                            store_pair_sums(TILES * n + s - 18, BLOCK * blk + (s - 18) * TILE)
                        if s == 12 and blk == 2 and not last:
                            erows(g + 1)
                        if s == 6 and blk == 3:
                            act.wait_ge(s_z0, n + 1)
                            if not first:
                                act.wait_ge(s_h1, g)
                            act.activation(z_top[:, 0, :], z0[:], ACT.Copy).then_inc(s_ztop, 1)
                        if not first:
                            if blk == 0 and s == 18:
                                store_z2(g - 1)
                            if blk == 1 and s == TOP1_AT[-1] + 1:
                                store_h1(g - 1)
                            if blk == 2 and s == 11:
                                store_h2(g - 1)
                            if blk == 3 and s == 8:
                                store_y(g - 1)

            group(0, True, False)
            with act.Fori(1, GROUPS - 1) as g:
                group(g, False, False)
            group(GROUPS - 1, False, True)
            for q in range(2):
                store_pair_sums(B // TILE - 2 + q, GROUP - (2 - q) * TILE)
            store_z1(GROUPS - 1)
            store_z2(GROUPS - 1)
            store_h1(GROUPS - 1)
            store_h2(GROUPS - 1)
            store_y(GROUPS - 1)

        @block.vector
        def _(dve):
            def product(m, c):
                k = CHUNKS0 * m + c
                first = isinstance(m, int) and m == 0
                if first:
                    dve.wait_ge(s_permuted, c + 1)
                else:
                    dve.wait_ge(s_shifted[c], 16 * len(shifts0(c)) * m)
                if c == 0:
                    dve.wait_ge(s_x0, m + 1)
                r = rows0(c)
                if c >= 2:
                    dve.wait_ge(s_low, k - 1)
                elif some(m):
                    dve.wait_ge(s_low, CHUNKS0 * m)
                src = parts[c % PARTS][0:r, :] if first else x0_shifted[0:r, c, :]
                dve.tensor_tensor(prods[c % 2][0:r, :], src, x0[0:r, :], ALU.mult).then_inc(s_prods, 1)

            def low(m, c):
                dve.wait_ge(s_high, CHUNKS0 * m + c + 1)
                dve.wait_ge(s_prods, CHUNKS0 * m + c + 1)
                r = rows0(c)
                dve.tensor_tensor(prods_lo[c % 2][0:r, :], prods[c % 2][0:r, :], prods_hi[c % 2][0:r, :].bitcast(F32),
                                  ALU.subtract).then_inc(s_low, 1)

            def split_x1(par, m):
                dve.wait_ge(s_x1, m + 1)
                dve.wait_ge(s_x1hi, m + 1)
                dve.tensor_tensor(x1_lo[par][:], x1[:], x1_hi[par][:].bitcast(F32),
                                  ALU.subtract).then_inc(s_x1lo, 1)

            def sum_x1(m, col):
                dve.tensor_reduce(z0[:, bass.ds(col, BLOCK)], x1[:].rearrange("p (b d) -> p b d", d=D),
                                  AX.X, ALU.add).then_inc(s_z0, 1)

            def fold_late(u, p, q):
                x = terms[p][q]
                dve.wait_ge(s_term, 2 * TERMS * (u + 1) - 3 * (1 - q))
                dve.wait_ge(s_acc, PER_PAIR * (u + 1) - 1 + q)
                dve.tensor_tensor(x[:, 12:16, :], x[:, 12:16, :], x[:, 16:20, :], ALU.add).then_inc(s_folds, 1)

            def add_terms(u, c, p, par):
                k = PER_PAIR * u + DVE_UPTO[c]
                for n, j in enumerate(FIELDS[c]):
                    for q in range(2):
                        if n == 0:
                            dve.wait_ge(s_part, 2 * (CHUNKS * u + c) + 1 + q)
                        if c or n:
                            dve.wait_ge(s_acc, k + 2 * n + q - 1)
                        total = terms[p][q][:, TERMS, :]
                        dve.scalar_tensor_tensor(
                            out=total, in0=parts[bank(c, q)][:, n * H:(n + 1) * H],
                            scalar=x0_t[par][:, 2 * p + q, j:j + 1], in1=total if c or n else bias1[:],
                            op0=ALU.mult, op1=ALU.add).then_inc(s_acc, 1)

            dve.wait_ge(s_w0, 32)
            dve.tensor_tensor(w0_raw, w0_raw, w0_mirror, ALU.add).then_inc(s_w0sum, 1)
            dve.wait_ge(s_w1hi, 1)
            dve.tensor_tensor(w1_lo[:], w1_raw[:, 0:NF, :], w1_hi[:].bitcast(F32), ALU.subtract).then_inc(s_w1lo, 1)
            dve.wait_ge(s_w0hi, 1)
            dve.tensor_tensor(w0_lo[:], w0_raw, w0_hi[:].bitcast(F32), ALU.subtract).then_inc(s_w0lo, 1)
            dve.wait_ge(s_x0hi, 1)
            dve.tensor_tensor(x0_lo[0:NF, :], x0[0:NF, :], x0_hi[0:NF, :].bitcast(F32),
                              ALU.subtract).then_inc(s_x0lo, 1)
            product(0, 0)
            for c in range(CHUNKS0):
                if c + 1 < CHUNKS0:
                    product(0, c + 1)
                low(0, c)
            split_x1(0, 0)
            sum_x1(0, 0)
            dve.wait_ge(s_const, 16 * 5)
            dve.wait_ge(s_x0t, 1)

            def group(g, first, last):
                for blk in range(BLOCKS):
                    n = BLOCKS * g + blk
                    more = not (last and blk == BLOCKS - 1)
                    for s in range(STEPS):
                        p, c = divmod(s, CHUNKS)
                        if c not in ACT_CHUNKS:
                            add_terms(PAIRS * n + p, c, p, blk % 2)
                        if c in (0, 2) and not (first and blk == 0 and p == 0):
                            fold_late(PAIRS * n + p - 1, 1 - p, c // 2)
                        if not more:
                            continue
                        if first and blk == 0 and s == 1:
                            product(1, 0)
                        if s in PRODUCT_AT:
                            product(n + 1, PRODUCT_AT[s])
                        if s in LOW_AT:
                            low(n + 1, LOW_AT[s])
                        if s == 16:
                            split_x1((blk + 1) % 2, n + 1)
                        if s == 18:
                            if blk == BLOCKS - 1:
                                dve.wait_ge(s_ztop, 2 * g + 1)
                            sum_x1(n + 1, BLOCK * ((blk + 1) % BLOCKS))
                        if s == 19 and not (last and blk >= BLOCKS - 2):
                            product(n + 2, 0)

            group(0, True, False)
            with dve.Fori(1, GROUPS - 1) as g:
                group(g, False, False)
            group(GROUPS - 1, False, True)
            for q in range(2):
                fold_late(PAIRS * BLOCKS * GROUPS - 1, 1, q)

        @block.tensor
        def _(pe):
            def turn_x0(blk, m):
                pe.wait_ge(s_erows, m // BLOCKS + 1 if isinstance(m, int) else erow_count[0])
                if some(m):
                    pe.wait_ge(s_x0t, m)
                if some(TILES * (m - 2)):
                    pe.wait_ge(s_p2out, TILES * (m - 2))
                pe.sem_inc(s_met, 1)
                r = slice(BLOCK * blk, BLOCK * (blk + 1))
                for d in range(D):
                    ins = pe.transpose(ps_misc[0:ROWS0, d * BLOCK:(d + 1) * BLOCK], e_rows[r, d, :], ident[r, r])
                ins.then_inc(s_turned, 1)

            def turn_x0t(m):
                pe.wait_ge(s_x0, m + 1)
                if some(TILES * (m - 1) - 2):
                    pe.wait_ge(s_p2out, TILES * (m - 1) - 2)
                pe.sem_inc(s_met, 1)
                for i in range(TILES):
                    ins = pe.transpose(ps_misc[:, i * NF:(i + 1) * NF], x0[0:NF, i * P:(i + 1) * P],
                                       ident[0:NF, 0:NF])
                ins.then_inc(s_turned_t, 1)

            def permute(c):
                if c == 0:
                    pe.wait_ge(s_x0hi, 1)
                    pe.wait_ge(s_permsr, 2)
                if c >= PARTS:
                    pe.wait_ge(s_prods, c - PARTS + 1)
                r = rows0(c)
                at = c % PERMS * ROWS0
                perm = perms[c // PERMS][0:NF, at:at + r]
                pe.matmul(parts[c % PARTS][0:r, :], perm, x0_hi[0:NF, :], start=True, stop=False)
                if c == 0:
                    pe.wait_ge(s_x0lo, 1)
                pe.matmul(parts[c % PARTS][0:r, :], perm, x0_lo[0:NF, :], start=False,
                          stop=True).then_inc(s_permuted, 1)

            def layer0(m, c):
                if c == 0 and some(m):
                    pe.wait_ge(s_x1, m)
                r = rows0(c)
                pe.wait_ge(s_high, CHUNKS0 * m + c + 1)
                pe.matmul(ps_x1[:], w0_hi[0:r, c, :], prods_hi[c % 2][0:r, :], start=(c == 0), stop=False)
                pe.matmul(ps_x1[:], w0_lo[0:r, c, :], prods_hi[c % 2][0:r, :], start=False, stop=False)
                pe.wait_ge(s_low, CHUNKS0 * m + c + 1)
                pe.matmul(ps_x1[:], w0_hi[0:r, c, :], prods_lo[c % 2][0:r, :], start=False,
                          stop=(c == CHUNKS0 - 1)).then_inc(s_l0, 1)

            def layer1(u, c, p, par):
                w = len(FIELDS[c]) * H
                f = slice(FIELDS[c][0], FIELDS[c][-1] + 1)
                for q in range(2):
                    q2 = 1 - q
                    back = (PARTS + 1 - 2 * q) // 2
                    c2, u2 = (c - back) % CHUNKS, u - (c < back)
                    if c2 in ACT_CHUNKS:
                        count = 2 * TERMS * u2 + ACT_UPTO[c2 + 1] - len(FIELDS[c2]) * (1 - q2)
                        if some(count):
                            pe.wait_ge(s_term, count)
                    else:
                        count = PER_PAIR * u2 + DVE_UPTO[c2 + 1] - 1 + q2
                        if some(count):
                            pe.wait_ge(s_acc, count)
                    out = parts[bank(c, q)][:, 0:w]
                    hi = x1_hi[par][:, tile(q, p)]
                    lo = x1_lo[par][:, tile(q, p)]
                    pe.matmul(out, hi, w1_hi[:, f, :], start=True, stop=False)
                    pe.matmul(out, hi, w1_lo[:, f, :], start=False, stop=False)
                    if c == 0 and p == 0 and q == 0:
                        pe.wait_ge(s_x1lo, u // PAIRS + 1 if isinstance(u, int) else block_count[0])
                    pe.matmul(out, lo, w1_hi[:, f, :], start=False, stop=True).then_inc(s_part, 1)

            def sum_pairs(i, par, k, p, q, m):
                pe.wait_ge(s_x2, i + 1)
                if some(i):
                    pe.wait_ge(s_p2out, i)
                pe.matmul(ps_misc[:, 0:NP2 * TILE], terms[p][q][:, 0, :],
                          x0_blocks[par][:, k, :, :].rearrange("p j b -> p (j b)"), start=True,
                          stop=True).then_inc(s_p2, 1)

            def z2(g, js):
                if js[0] == 0:
                    pe.wait_ge(s_p2out, (g + 1) * GROUP // TILE)
                    if some(g):
                        pe.wait_ge(s_yout, g)
                for j in js:
                    ins = pe.matmul(ps_top[:, 0:GROUP], w2[:, j, :], pair_sums[:, j, :], start=(j == 0),
                                    stop=(j == NF - 1))
                if js[-1] == NF - 1:
                    ins.then_inc(s_z2, 1)

            def top1(g, i, last):
                if i == 0:
                    pe.wait_ge(s_z2out, g + 1)
                    pe.wait_ge(s_ztop, 2 * g + 2)
                    pe.wait_ge(s_dense, 16 * (g + 1))
                out = ps_top[:, i * GROUP:(i + 1) * GROUP]
                for k in range(3):
                    pe.matmul(out, wt1[:, k, i * P:(i + 1) * P], z_top[:, k, :], start=(k == 0), stop=False)
                ins = pe.matmul(out, wt1_dense[:, i * P:(i + 1) * P], dense[:], start=False, stop=True)
                if i == 3:
                    ins.then_inc(s_h1, 1)

            def top2(g, i):
                if i == 0:
                    pe.wait_ge(s_h1out, 4 * (g + 1))
                for k in range(4):
                    ins = pe.matmul(ps_top[:, i * GROUP:(i + 1) * GROUP], wt2[:, k, i * P:(i + 1) * P],
                                    h1[:, k, :], start=(k == 0), stop=(k == 3))
                if i == 1:
                    ins.then_inc(s_h2, 1)

            def top3(g):
                pe.wait_ge(s_h2out, 2 * (g + 1))
                for k in range(2):
                    ins = pe.matmul(ps_top[0:1, 0:GROUP], wt3[:, k:k + 1], h2[:, k, :], start=(k == 0),
                                    stop=(k == 1))
                ins.then_inc(s_y, 1)

            def stay_warm(count):
                for _ in range(count):
                    pe.matmul(ps_top[:], w1_hi[:, 0, :], w1_hi[:, 0:COLS // H, :], start=True, stop=True)

            erow_count = [1]
            block_count = [1]
            pe.wait_ge(s_const, 16 * 5)
            pe.wait_ge(s_w1hi, 1)
            pe.wait_ge(s_ones, 1)
            stay_warm(51)
            turn_x0(0, 0)
            stay_warm(7)
            permute(0)
            permute(1)
            turn_x0t(0)
            for c in range(2, PARTS):
                permute(c)
            pe.wait_ge(s_w0lo, 1)
            pe.wait_ge(s_w0sum, 1)
            for c in range(CHUNKS0):
                if 0 < c < CHUNKS0 - PARTS + 1:
                    permute(c + PARTS - 1)
                layer0(0, c)
                stay_warm(2)
            turn_x0(1, 1)
            stay_warm(2)
            pe.wait_ge(s_x1hi, 1)
            pe.wait_ge(s_w1lo, 1)
            pe.wait_ge(s_top_w, 16 * 7)

            Z2_STEP = 6

            def group(g, first, last):
                for blk in range(BLOCKS):
                    n = BLOCKS * g + blk
                    more = not (last and blk == BLOCKS - 1)
                    par, nxt = blk % 2, (blk + 1) % 2
                    erow_count[0] = g + 1 + (blk + 2) // BLOCKS
                    block_count[0] = n + 1
                    for s in range(STEPS):
                        p, c = divmod(s, CHUNKS)
                        layer1(PAIRS * n + p, c, p, par)
                        if s == 15 and not (last and blk >= BLOCKS - 2):
                            turn_x0((blk + 2) % BLOCKS, n + 2)
                        if more:
                            for c0 in LAYER0_AT.get(s, ()):
                                layer0(n + 1, c0)
                        if s in (8, 10) and not (first and blk == 0):
                            if s == 8 and more:
                                pe.wait_ge(s_x0t, n + 2)
                            sum_pairs(TILES * n - 6 + s // 2, nxt, s // 2 - 2, 1, s // 2 - 4, n - 1)
                        if s == 3 and more:
                            turn_x0t(n + 1)
                        if s in (18, 19):
                            if s == 18:
                                pe.wait_ge(s_blocks, n + 1)
                                if not (last and blk >= BLOCKS - 2):
                                    pe.wait_ge(s_x0, n + 3)
                            sum_pairs(TILES * n + s - 18, par, s - 18, 0, s - 18, n)
                        if not first:
                            if blk == 0 and 11 <= s < 18:
                                z2(g - 1, range((s - 11) * Z2_STEP, min(NF, (s - 10) * Z2_STEP)))
                            if blk == 1 and s in TOP1_AT:
                                top1(g - 1, TOP1_AT.index(s), last)
                            if blk == 2 and s in (5, 7):
                                top2(g - 1, (s - 5) // 2)
                            if blk == 3 and s == 5:
                                top3(g - 1)
                    if more:
                        pe.wait_ge(s_x1hi, n + 2)

            group(0, True, False)
            with pe.Fori(1, GROUPS - 1) as g:
                group(g, False, False)
            group(GROUPS - 1, False, True)
            g = GROUPS - 1
            pe.wait_ge(s_yout, GROUPS - 1)
            stay_warm(20)
            for q in range(2):
                sum_pairs(B // TILE - 2 + q, 1, 2 + q, 1, q, 0)
            z2(g, range(NF))
            for i in range(4):
                top1(g, i, True)
            for i in range(2):
                top2(g, i)
            top3(g)


def kernel(**inputs):
    import concourse.bacc as bacc
    from concourse.bass_utils import run_bass_kernel_spmd as run

    x = {k: np.asarray(v) for k, v in inputs.items()}
    first = np.tile(np.arange(NF), 3 * CHUNKS0)
    shift = np.repeat(np.arange(3 * CHUNKS0), NF)
    second = (first + shift) % NF
    W0 = x["L0_rec_W0"].reshape(H, NF, NF)
    used = (shift < SHIFTS)[:, None]
    w0 = np.where(used, W0[:, first, second].T, np.float32(0))
    mirror = np.where(used & (shift > 0)[:, None], W0[:, second, first].T, np.float32(0))

    def chunks0(a):
        return a.reshape(CHUNKS0, ROWS0, H).transpose(1, 0, 2)

    arrays = {
        "ids": x["ids"],
        "dense": x["dense_ctx"].T,
        "ident": np.eye(P, dtype=np.float32),
        "own_row": np.repeat(np.eye(TILE, dtype=np.float32), D, axis=0),
        "w0": chunks0(w0),
        "w0_mirror": chunks0(mirror),
        "perms": (np.arange(NF)[:, None] == second[None]).astype(np.float32).reshape(NF, CHUNKS0, ROWS0),
        "w1": x["L0_rec_W1"].reshape(H, NF, H).transpose(2, 1, 0),
        "w2": x["L0_rec_W2"].reshape(H, NF, H).transpose(2, 1, 0),
        "b0": x["L0_rec_b0"].reshape(H, 1),
        "b1": x["L0_rec_b1"].reshape(1, H),
        "b2": x["L0_rec_b2"].reshape(H, 1),
        "wt1": x["W_top1"][:3 * P].reshape(3, P, 512).transpose(1, 0, 2),
        "wt1_dense": x["W_top1"][3 * P:],
        "wt2": x["W_top2"].reshape(4, P, 256).transpose(1, 0, 2),
        "wt3": x["W_top3"].reshape(2, P).T,
        "bt1": x["b_top1"].reshape(4, P).T,
        "bt2": x["b_top2"].reshape(2, P).T,
    }
    arrays.update({f"tbl_{f}": x[f"tbl_{f}"] for f in range(NF)})
    nc = bacc.Bacc("TRN2", target_bir_lowering=False, num_devices=1)
    given, t = {}, {}
    for name, a in arrays.items():
        a = np.ascontiguousarray(a)
        given[f"in_{name}"] = a
        t[name] = nc.dram_tensor(f"in_{name}", a.shape, mybir.dt.from_np(a.dtype), kind="ExternalInput").ap()
    t["y"] = nc.dram_tensor("out_y", (1, B), F32, kind="ExternalOutput").ap()
    build(nc, t)
    r = run(nc, [given], core_ids=[0])
    return r.results[0]["out_y"].reshape(B, 1)
```
